# Optimizing a Trainium2 kernel written in Bass

```python
import numpy as np
import jax
import jax.numpy as jnp

def _softmax(x, axis=-1):
    return jax.nn.softmax(x, axis=axis)

def _gelu(x):
    return jax.nn.gelu(x, approximate=True)

def _silu(x):
    return jax.nn.silu(x)

def _sigmoid(x):
    return jax.nn.sigmoid(x)

def _layernorm(x, axis=-1, eps=1e-05):
    m = jnp.mean(x, axis=axis, keepdims=True)
    v = jnp.var(x, axis=axis, keepdims=True)
    return (x - m) / jnp.sqrt(v + eps)

def _scatter_add(tgt, idx, src, axis=0):
    return tgt.at[idx].add(src)

def _segment_sum(src, seg, n):
    return jax.ops.segment_sum(src, seg, n)
kernel_name = 'mk_cond_resid_d2_seqx_r4_7a098a'

def setup_inputs(seed: int=0):
    np.random.seed(seed)
    _w = jnp.asarray

    def _rec_inputs():
        import jax
        import jax.numpy as jnp
        _rk = jax.random.key(seed)
        x = -0.0002071 + 1 * jax.random.normal(jax.random.fold_in(_rk, 1), (8, 256, 256), jnp.float32)
        _lenS = 256 - jax.random.randint(jax.random.fold_in(_rk, 7), (8,), 0, max(1, 256 // 4) + 1, jnp.int32)
        _lenS2 = 256 - jax.random.randint(jax.random.fold_in(_rk, 8), (8,), 0, max(1, 256 // 4) + 1, jnp.int32)
        cond_8 = jax.random.uniform(jax.random.fold_in(_rk, 11), (8, 8), jnp.float32, 0.0, 0.983423)
        return (x, cond_8)
    x, cond_8 = _rec_inputs()

    def _L0_cond_setup():
        import jax, jax.numpy as jnp
        import numpy as np
        R = 16
        ALPHA = 32.0
        SCALING = ALPHA / R
        key = jax.random.key(seed)
        ks = jax.random.split(key, 6)
        B, T, C, O, E = (16, 375, 256, 256, 8)
        x = jax.random.normal(ks[0], (B, T, C), dtype=jnp.float32)
        w = jax.random.uniform(ks[1], (B, E), dtype=jnp.float32)
        W_base = jax.random.normal(ks[2], (O, C), dtype=jnp.float32) * 0.02
        b_base = jax.random.normal(ks[3], (O,), dtype=jnp.float32) * 0.02
        As = jax.random.normal(ks[4], (E, R, C), dtype=jnp.float32) * 0.02
        Bs = jax.random.normal(ks[5], (E, O, R), dtype=jnp.float32) * 0.02
        return {'x': x, 'w': w, 'W_base': W_base, 'b_base': b_base, 'As': As, 'Bs': Bs}
    _L0_cond_all = _L0_cond_setup()
    _L0_cond_in = {k: v for k, v in _L0_cond_all.items() if k in ('W_base', 'b_base', 'As', 'Bs')}
    del _L0_cond_all

    def _L1_cond_setup():
        import jax, jax.numpy as jnp
        import numpy as np
        TOP_K = 2
        NUM_MOE_LAYERS = 12

        def _gemma_mlp(x, gate_w, up_w, down_w):
            g = jnp.einsum('bsh,hi->bsi', x, gate_w)
            u = jnp.einsum('bsh,hi->bsi', x, up_w)
            return jnp.einsum('bsi,ih->bsh', jax.nn.gelu(g, approximate=True) * u, down_w)
        key = jax.random.key(seed)
        ks = jax.random.split(key, 8)
        B, S, H, I, E = (32, 64, 256, 1024, 8)
        std = 0.02
        return {'x': jax.random.normal(ks[0], (B, S, H), jnp.float32), 'router_logits': jax.random.normal(ks[1], (B, E), jnp.float32), 'skill_gate': jax.random.normal(ks[2], (E, H, I), jnp.float32) * std, 'skill_up': jax.random.normal(ks[3], (E, H, I), jnp.float32) * std, 'skill_down': jax.random.normal(ks[4], (E, I, H), jnp.float32) * std, 'shared_gate': jax.random.normal(ks[5], (H, I), jnp.float32) * std, 'shared_up': jax.random.normal(ks[6], (H, I), jnp.float32) * std, 'shared_down': jax.random.normal(ks[7], (I, H), jnp.float32) * std}
    _L1_cond_all = _L1_cond_setup()
    _L1_cond_in = {k: v for k, v in _L1_cond_all.items() if k in ('skill_gate', 'skill_up', 'skill_down', 'shared_gate', 'shared_up', 'shared_down')}
    del _L1_cond_all
    return {'x': x, 'cond_8': cond_8, 'L0_cond_W_base': _L0_cond_in['W_base'], 'L0_cond_b_base': _L0_cond_in['b_base'], 'L0_cond_As': _L0_cond_in['As'], 'L0_cond_Bs': _L0_cond_in['Bs'], 'L1_cond_skill_gate': _L1_cond_in['skill_gate'], 'L1_cond_skill_up': _L1_cond_in['skill_up'], 'L1_cond_skill_down': _L1_cond_in['skill_down'], 'L1_cond_shared_gate': _L1_cond_in['shared_gate'], 'L1_cond_shared_up': _L1_cond_in['shared_up'], 'L1_cond_shared_down': _L1_cond_in['shared_down']}

def reference(x, cond_8, L0_cond_W_base, L0_cond_b_base, L0_cond_As, L0_cond_Bs, L1_cond_skill_gate, L1_cond_skill_up, L1_cond_skill_down, L1_cond_shared_gate, L1_cond_shared_up, L1_cond_shared_down):
    import jax
    import jax.numpy as jnp

    def _L0_cond_ref(x, w, W_base, b_base, As, Bs):
        import jax, jax.numpy as jnp
        import numpy as np
        R = 16
        ALPHA = 32.0
        SCALING = ALPHA / R
        out = jnp.einsum('btc,oc->bto', x, W_base) + b_base
        h = jnp.einsum('btc,erc->bter', x, As)
        lora = jnp.einsum('bter,eor,be->bto', h, Bs, w)
        return out + lora * SCALING

    def _L1_cond_ref(x, router_logits, skill_gate, skill_up, skill_down, shared_gate, shared_up, shared_down):
        import jax, jax.numpy as jnp
        import numpy as np
        TOP_K = 2
        NUM_MOE_LAYERS = 12

        def _gemma_mlp(x, gate_w, up_w, down_w):
            g = jnp.einsum('bsh,hi->bsi', x, gate_w)
            u = jnp.einsum('bsh,hi->bsi', x, up_w)
            return jnp.einsum('bsi,ih->bsh', jax.nn.gelu(g, approximate=True) * u, down_w)
        B = x.shape[0]
        E = skill_gate.shape[0]
        rw = jax.nn.softmax(router_logits.astype(jnp.float32), axis=-1)
        w, sel = jax.lax.top_k(rw, TOP_K)
        w = w / w.sum(axis=-1, keepdims=True)
        w = w.astype(x.dtype)
        scale = 1.0 / NUM_MOE_LAYERS
        w = scale * w + (1.0 - scale) * jax.lax.stop_gradient(w)
        dense_w = jnp.zeros((B, E), x.dtype).at[jnp.arange(B)[:, None], sel].add(w)

        def step(acc, params):
            g, u, d, we = params
            return (acc + we[:, None, None] * _gemma_mlp(x, g, u, d), None)
        out, _ = jax.lax.scan(step, jnp.zeros_like(x), (skill_gate, skill_up, skill_down, dense_w.T))
        out = out + _gemma_mlp(x, shared_gate, shared_up, shared_down)
        return out
    x = x + _L0_cond_ref(x, cond_8, L0_cond_W_base, L0_cond_b_base, L0_cond_As, L0_cond_Bs)
    x = x + _L1_cond_ref(x, cond_8, L1_cond_skill_gate, L1_cond_skill_up, L1_cond_skill_down, L1_cond_shared_gate, L1_cond_shared_up, L1_cond_shared_down)
    return x

_drawn_inputs = setup_inputs


def setup_inputs(seed=0):
    import zlib

    import numpy as np

    out = dict(_drawn_inputs(seed))
    spreads = {}
    factors = {'L0_cond_b_base': 3.245}
    for name, (base, spread) in spreads.items():
        noise = np.random.default_rng([zlib.crc32(name.encode()), seed]).standard_normal(out[name].shape)
        drawn = base * np.exp(spread * noise) if base else spread * noise
        out[name] = jnp.asarray(drawn.astype(out[name].dtype))
    for name, factor in factors.items():
        out[name] = (out[name] * factor).astype(out[name].dtype)
    return out
```

```python
from contextlib import ExitStack

import concourse.bass as bass
from concourse import mybir


def cond_resid_kernel(nc, xT, cond, condT, base_wT, base_b, lora_aT, lora_bT, experts, shared, outT):
    F32, F32R, I32 = mybir.dt.float32, mybir.dt.float32r, mybir.dt.int32
    ALU, ACT, AX = mybir.AluOpType, mybir.ActivationFunctionType, mybir.AxisListType

    P = 128
    H, TOKENS = xT.shape
    B, E = cond.shape
    KH = H // P
    T = TOKENS // B
    PT = 2 * T
    PAIRS = B // 2
    ER = lora_aT.shape[1]
    CHUNKS = shared.shape[0] // P
    CW = shared.shape[1]
    QUARTERS = experts.shape[0] // (E * P)
    QC = CHUNKS // QUARTERS
    QW = QC * CW
    ROUTED = 2 * 2 * QUARTERS
    PER_S = ROUTED // CHUNKS
    STEPS = CHUNKS + ROUTED
    LORA_SCALE = 32.0 / 16.0
    MIX = 1.0 / 12.0
    GATE, UP, DOWN = 0, H, 2 * H
    assert ER == P and PT == 512 and QC * T == PT and CW == 3 * H

    LAG = 2
    HB = 3
    RAW = 4
    SPLIT = 4
    AHEAD = 2
    SRAW = 2
    NUMBERS_AT = 17
    X_AT, H_AT, HS_AT, O_AT, X1_AT = 3, 4, 6, 7, 9

    def step_of(r):
        return (PER_S + 1) * (r // PER_S) + 1 + r % PER_S

    def done_steps(it, s, back):
        n = it * STEPS + (s - back + 1)
        return None if isinstance(n, int) and n <= 0 else n

    KINDS = []
    for j in range(CHUNKS):
        KINDS += [(True, j)] + [(False, j * PER_S + i) for i in range(PER_S)]

    ctx = ExitStack()
    with ctx:
        def sb(name, shape, dt=F32):
            return ctx.enter_context(nc.sbuf_tensor(name, shape, dt))

        def sem(name):
            return ctx.enter_context(nc.semaphore(name))

        x_in = sb("x_in", [P, KH * PT])
        x_hi, x_lo = sb("x_hi", [P, KH * PT], F32R), sb("x_lo", [P, KH * PT], F32R)
        l0_w = sb("l0_w", [P, KH * H + KH * ER + H])
        l0_hi, l0_lo = sb("l0_hi", list(l0_w.shape), F32R), sb("l0_lo", list(l0_w.shape), F32R)
        bias = sb("bias", [P, KH])
        lora_mix = sb("lora_mix", [P, B])
        lora = sb("lora", [P, PT])
        lora_hi, lora_lo = sb("lora_hi", [P, PT], F32R), sb("lora_lo", [P, PT], F32R)
        x1 = sb("x1", [P, 2 * KH * PT])
        x1_hi, x1_lo = sb("x1_hi", [P, 2 * KH * PT], F32R), sb("x1_lo", [P, 2 * KH * PT], F32R)
        logits = sb("logits", [P, B, E])
        rank = sb("rank", [P, B, E])
        shifted, prob, rest, mark, mark_b = (sb(n, [P, B, E]) for n in ("shifted", "prob", "rest", "mark", "mark_b"))
        top_logit, total, top_a, top_b, rank_a, rank_b, both = (
            sb(n, [P, B, 1]) for n in ("top_logit", "total", "top_a", "top_b", "rank_a", "rank_b", "both"))
        share, share_mix, route_w = (sb(n, [P, B, 2]) for n in ("share", "share_mix", "route_w"))
        route_e = sb("route_e", [P, B * 2], I32)
        s_raw = sb("s_raw", [P, SRAW, CW])
        s_hi, s_lo = sb("s_hi", [P, CHUNKS, CW], F32R), sb("s_lo", [P, CHUNKS, CW], F32R)
        w_raw = sb("w_raw", [P, RAW, QW])
        w_hi, w_lo = sb("w_hi", [P, SPLIT, QW], F32R), sb("w_lo", [P, SPLIT, QW], F32R)
        gelu = sb("gelu", [P, 2, PT])
        hid = sb("hid", [P, 2, PT])
        hid_hi, hid_lo = sb("hid_hi", [P, HB, PT], F32R), sb("hid_lo", [P, HB, PT], F32R)
        y = sb("y", [P, KH, PT])

        def bank(name):
            return ctx.enter_context(nc.psum_tensor(name, [P, PT], F32))

        gate_ps = [bank(f"gate_ps{i}") for i in range(2)]
        up_ps = [bank(f"up_ps{i}") for i in range(2)]
        out_ps = [bank(f"out_ps{m}") for m in range(KH)]
        l0_ps = [bank(f"l0_ps{m}") for m in range(2)]

        cond_loaded = sem("cond_loaded")
        l0_loaded = sem("l0_loaded")
        small_loaded = sem("small_loaded")
        x_loaded = sem("x_loaded")
        s_loaded = [sem(f"s_loaded{i}") for i in range(SRAW)]
        w_loaded = [sem(f"w_loaded{i}") for i in range(RAW)]
        rank_set = sem("rank_set")
        routing = sem("routing")
        shifted_exp = sem("shifted_exp")
        l0_hi_done, l0_lo_done = sem("l0_hi_done"), sem("l0_lo_done")
        x_hi_done, x_lo_done = sem("x_hi_done"), sem("x_lo_done")
        lora_ready = sem("lora_ready")
        lora_done = sem("lora_done")
        lora_hi_done, lora_lo_done = sem("lora_hi_done"), sem("lora_lo_done")
        l0_ready = sem("l0_ready")
        x1_done, x1_hi_done, x1_lo_done = sem("x1_done"), sem("x1_hi_done"), sem("x1_lo_done")
        s_hi_done, s_lo_done = sem("s_hi_done"), sem("s_lo_done")
        w_hi_done, w_lo_done = sem("w_hi_done"), sem("w_lo_done")
        gate_ready, up_ready, gelu_done = sem("gate_ready"), sem("up_ready"), sem("gelu_done")
        hid_done, hid_hi_done, hid_lo_done = sem("hid_done"), sem("hid_hi_done"), sem("hid_lo_done")
        down_done = sem("down_done")
        out_ready = sem("out_ready")
        y_done = sem("y_done")
        y_stored = [sem(f"y_stored{m}") for m in range(KH)]

        BASE_AT, A_AT, B_AT = 0, KH * H, KH * H + KH * ER

        xT_v = xT.rearrange("(k p) t -> p k t", p=P)
        outT_v = outT.rearrange("(k p) t -> p k t", p=P)

        def parity(it):
            return it % 2 if isinstance(it, int) else it & 1

        def x1_cols(it, col, n):
            start = parity(it) * (KH * PT) + col
            return slice(start, start + n) if isinstance(start, int) else bass.ds(start, n)

        def cols(start, n):
            return slice(start, start + n) if isinstance(start, int) else bass.ds(start, n)

        block = ctx.enter_context(nc.Block())

        @block.sync
        def _(sp):
            def load_x(it):
                if not isinstance(it, int) or it >= 1:
                    sp.wait_ge(x1_done, it * KH)
                sp.dma_start(x_in[:].rearrange("p (k t) -> p k t", k=KH),
                             xT_v[:, :, cols(it * PT, PT)]).then_inc(x_loaded, 16)

            def load_shared(j):
                if j >= SRAW:
                    sp.wait_ge(s_lo_done, j - SRAW + 1)
                sp.dma_start(s_raw[:, j % SRAW, :], shared[j * P:(j + 1) * P, :]).then_inc(s_loaded[j % SRAW], 16)

            def load_pair(it, first=False, last=False):
                if not last:
                    load_x(it + 1)
                for r in range(ROUTED):
                    if r % QUARTERS == 0:
                        e = sp.value_load(route_e[0:1, cols(it * 4 + r // QUARTERS, 1)], min_val=0, max_val=E - 1)
                        row = sp.snap(e * (QUARTERS * P))
                    if first and r % PER_S == 0 and 2 + r // PER_S < CHUNKS:
                        load_shared(2 + r // PER_S)
                    if not first or r >= RAW:
                        sp.wait_ge(w_lo_done, it * ROUTED + (r - RAW + 1))
                    sp.dma_start(w_raw[:, r % RAW, :], experts[bass.ds(row + (r % QUARTERS) * P, P), :]) \
                      .then_inc(w_loaded[r % RAW], 16)

            load_x(0)
            load_shared(0)
            load_shared(1)
            sp.wait_ge(routing, NUMBERS_AT)
            load_pair(0, first=True)
            with sp.Fori(1, PAIRS - 1) as it:
                load_pair(it)
            load_pair(PAIRS - 1, last=True)

        @block.gpsimd
        def _(pool):
            for e in range(E - 1):
                nc.gpsimd.memset(rank[:, :, e:e + 1], float(E - e))
            nc.gpsimd.memset(rank[:, :, E - 1:E], 1.0).then_inc(rank_set, 1)
            with pool.Fori(0, PAIRS) as it:
                for m in range(KH):
                    pool.wait_ge(y_done, it * KH + (m + 1))
                    pool.dma_start(outT_v[:, m, bass.ds(it * PT, PT)], y[:, m, :]).then_inc(y_stored[m], 16)
            for m in range(KH):
                pool.wait_ge(y_stored[m], 16 * PAIRS)

        @block.scalar
        def _(act):
            act.dma_start(logits[:], cond.rearrange("(o b) e -> o b e", o=1).broadcast_to([P, B, E])) \
               .then_inc(cond_loaded, 16)
            act.dma_start(l0_w[:, A_AT:B_AT].rearrange("p (k n) -> p k n", k=KH),
                          lora_aT.rearrange("(k p) n -> p k n", p=P)).then_inc(l0_loaded, 16)
            act.dma_start(l0_w[:, BASE_AT:A_AT].rearrange("p (k n) -> p k n", k=KH),
                          base_wT.rearrange("(k p) n -> p k n", p=P)).then_inc(l0_loaded, 16)
            act.dma_start(l0_w[:, B_AT:], lora_bT).then_inc(l0_loaded, 16)
            act.dma_start(lora_mix[:], condT).then_inc(small_loaded, 16)
            act.dma_start(bias[:], base_b).then_inc(small_loaded, 16)

            act.wait_ge(routing, 2)
            nc.scalar.activation(shifted[:], shifted[:], ACT.Exp).then_inc(shifted_exp, 1)

            def x_part(it):
                act.wait_ge(x_loaded, 16 * (it + 1))
                if not isinstance(it, int) or it >= 1:
                    act.wait_ge(l0_ready, it * KH)
                nc.scalar.activation(x_hi[:], x_in[:], ACT.Copy).then_inc(x_hi_done, 1)

            def lora_part(it):
                act.wait_ge(lora_done, it + 1)
                nc.scalar.activation(lora_hi[:], lora[:], ACT.Copy).then_inc(lora_hi_done, 1)

            def x1_part(it):
                act.wait_ge(x1_done, it * KH + KH)
                nc.scalar.activation(x1_hi[:, x1_cols(it, 0, KH * PT)], x1[:, x1_cols(it, 0, KH * PT)], ACT.Copy) \
                  .then_inc(x1_hi_done, 1)

            def shared_part(j):
                act.wait_ge(s_loaded[j % SRAW], 16 * (j // SRAW + 1))
                nc.scalar.activation(s_hi[:, j, :], s_raw[:, j % SRAW, :], ACT.Copy).then_inc(s_hi_done, 1)

            def quarter_part(it, r, known_free=False):
                act.wait_ge(w_loaded[r % RAW], it * (16 * ROUTED // RAW) + 16 * (r // RAW + 1))
                if r >= SPLIT:
                    act.wait_ge(down_done, it * STEPS + (step_of(r - SPLIT) + 1))
                elif not known_free:
                    act.wait_ge(down_done, it * STEPS + (step_of(r - SPLIT + ROUTED) + 1 - STEPS))
                nc.scalar.activation(w_hi[:, r % SPLIT, :], w_raw[:, r % RAW, :], ACT.Copy).then_inc(w_hi_done, 1)

            def pair(it, first=False, last=False):
                for s, (is_shared, n) in enumerate(KINDS):
                    act.wait_ge(gate_ready, it * STEPS + (s + 1))
                    if not first or s >= 2:
                        act.wait_ge(hid_done, it * STEPS + (s - 1))
                    nc.scalar.activation(gelu[:, s % 2, :], gate_ps[s % 2][:], ACT.Gelu_apprx_tanh) \
                      .then_inc(gelu_done, 1)
                    if is_shared:
                        if first and n + 1 < CHUNKS:
                            shared_part(n + 1)
                    elif n + AHEAD < ROUTED:
                        quarter_part(it, n + AHEAD, known_free=first)
                    elif not last:
                        quarter_part(it + 1, n + AHEAD - ROUTED)
                    act.wait_ge(hid_done, it * STEPS + (s + 1))
                    if not first or s >= HB:
                        act.wait_ge(down_done, it * STEPS + (s - HB + 1))
                    nc.scalar.activation(hid_hi[:, s % HB, :], hid[:, s % 2, :], ACT.Copy).then_inc(hid_hi_done, 1)
                    if not last:
                        if s == X_AT:
                            x_part(it + 1)
                        if s == HS_AT:
                            lora_part(it + 1)
                        if s == X1_AT:
                            x1_part(it + 1)

            act.wait_ge(l0_loaded, 48)
            nc.scalar.activation(l0_hi[:], l0_w[:], ACT.Copy).then_inc(l0_hi_done, 1)
            x_part(0)
            lora_part(0)
            shared_part(0)
            x1_part(0)
            quarter_part(0, 0, known_free=True)
            quarter_part(0, 1, known_free=True)
            pair(0, first=True)
            with act.Fori(1, PAIRS - 1) as it:
                pair(it)
            pair(PAIRS - 1, last=True)

        @block.vector
        def _(dve):
            route_n = [0]

            def link(ins):
                route_n[0] += 1
                ins.then_inc(routing, 1)
                dve.wait_ge(routing, route_n[0])

            def over_e(t):
                return t[:].broadcast_to([P, B, E])

            dve.wait_ge(cond_loaded, 16)
            link(nc.vector.tensor_reduce(top_logit[:], logits[:], AX.X, ALU.max))
            link(nc.vector.tensor_tensor(shifted[:], logits[:], over_e(top_logit), ALU.subtract))
            dve.wait_ge(shifted_exp, 1)
            link(nc.vector.tensor_reduce(total[:], shifted[:], AX.X, ALU.add))
            link(nc.vector.reciprocal(total[:], total[:]))
            link(nc.vector.tensor_tensor(prob[:], shifted[:], over_e(total), ALU.mult))
            dve.wait_ge(rank_set, 1)
            link(nc.vector.tensor_reduce(top_a[:], prob[:], AX.X, ALU.max))
            link(nc.vector.tensor_tensor(mark[:], prob[:], over_e(top_a), ALU.is_equal))
            link(nc.vector.tensor_tensor(mark[:], mark[:], rank[:], ALU.mult))
            link(nc.vector.tensor_reduce(rank_a[:], mark[:], AX.X, ALU.max))
            link(nc.vector.tensor_tensor(mark_b[:], rank[:], over_e(rank_a), ALU.is_equal))
            link(nc.vector.scalar_tensor_tensor(rest[:], mark_b[:], -2.0, prob[:], ALU.mult, ALU.add))
            link(nc.vector.tensor_reduce(top_b[:], rest[:], AX.X, ALU.max))
            link(nc.vector.tensor_tensor(mark[:], rest[:], over_e(top_b), ALU.is_equal))
            link(nc.vector.tensor_tensor(mark[:], mark[:], rank[:], ALU.mult))
            link(nc.vector.tensor_reduce(rank_b[:], mark[:], AX.X, ALU.max))
            picks = route_e[:].rearrange("p (b n) -> p b n", n=2)
            link(nc.vector.tensor_scalar(picks[:, :, 0:1], rank_a[:], -1.0, float(E), ALU.mult, ALU.add))
            link(nc.vector.tensor_scalar(picks[:, :, 1:2], rank_b[:], -1.0, float(E), ALU.mult, ALU.add))
            assert route_n[0] == NUMBERS_AT
            link(nc.vector.tensor_tensor(both[:], top_a[:], top_b[:], ALU.add))
            link(nc.vector.reciprocal(both[:], both[:]))
            link(nc.vector.tensor_tensor(share[:, :, 0:1], top_a[:], both[:], ALU.mult))
            link(nc.vector.tensor_tensor(share[:, :, 1:2], top_b[:], both[:], ALU.mult))
            link(nc.vector.tensor_scalar(share_mix[:], share[:], 1.0 - MIX, None, ALU.mult))
            link(nc.vector.scalar_tensor_tensor(route_w[:], share[:], MIX, share_mix[:], ALU.mult, ALU.add))
            weight_of = route_w[:].rearrange("p b n -> p (b n)")

            def lo_part(out, value, hi):
                return nc.vector.tensor_tensor(out, value, hi.bitcast(F32), ALU.subtract)

            def x_part(it):
                dve.wait_ge(x_hi_done, it + 1)
                lo_part(x_lo[:], x_in[:], x_hi[:]).then_inc(x_lo_done, 1)

            def lora_part(it):
                dve.wait_ge(lora_ready, it + 1)
                if not isinstance(it, int) or it >= 1:
                    dve.wait_ge(lora_hi_done, it)
                for i in range(2):
                    ins = nc.vector.tensor_scalar(lora[:, i * T:(i + 1) * T], l0_ps[0][:, i * T:(i + 1) * T],
                                                  lora_mix[:, cols(it * 2 + i, 1)], LORA_SCALE, ALU.mult, ALU.mult)
                ins.then_inc(lora_done, 1)
                dve.wait_ge(lora_hi_done, it + 1)
                lo_part(lora_lo[:], lora[:], lora_hi[:]).then_inc(lora_lo_done, 1)

            def x1_part(it):
                for m in range(KH):
                    dve.wait_ge(l0_ready, it * KH + (m + 1))
                    nc.vector.scalar_tensor_tensor(x1[:, x1_cols(it, m * PT, PT)], l0_ps[1 - m][:], bias[:, m:m + 1],
                                                   x_in[:, m * PT:(m + 1) * PT], ALU.add, ALU.add) \
                      .then_inc(x1_done, 1)
                dve.wait_ge(x1_hi_done, it + 1)
                lo_part(x1_lo[:, x1_cols(it, 0, KH * PT)], x1[:, x1_cols(it, 0, KH * PT)],
                        x1_hi[:, x1_cols(it, 0, KH * PT)]).then_inc(x1_lo_done, 1)

            def shared_part(j):
                dve.wait_ge(s_hi_done, j + 1)
                lo_part(s_lo[:, j, :], s_raw[:, j % SRAW, :], s_hi[:, j, :]).then_inc(s_lo_done, 1)

            def quarter_part(it, r):
                dve.wait_ge(w_hi_done, it * ROUTED + (r + 1))
                lo_part(w_lo[:, r % SPLIT, :], w_raw[:, r % RAW, :], w_hi[:, r % SPLIT, :]).then_inc(w_lo_done, 1)

            def residual(it, m):
                if m < KH - 1:
                    dve.wait_ge(out_ready, it * (KH - 1) + (m + 1))
                else:
                    dve.wait_ge(down_done, it * STEPS + STEPS)
                if not isinstance(it, int) or it >= 1:
                    dve.wait_ge(y_stored[m], 16 * it)
                nc.vector.tensor_tensor(y[:, m, :], out_ps[m][:], x1[:, x1_cols(it, m * PT, PT)], ALU.add) \
                  .then_inc(y_done, 1)

            def pair(it, first=False, last=False):
                for s, (is_shared, n) in enumerate(KINDS):
                    dve.wait_ge(gelu_done, it * STEPS + (s + 1))
                    dve.wait_ge(up_ready, it * STEPS + (s + 1))
                    if not first or s >= 2:
                        dve.wait_ge(hid_lo_done, it * STEPS + (s - 1))
                    if is_shared:
                        ins = nc.vector.tensor_tensor(hid[:, s % 2, :], gelu[:, s % 2, :], up_ps[s % 2][:], ALU.mult)
                    else:
                        w = weight_of[:, cols(it * 4 + n // QUARTERS, 1)]
                        ins = nc.vector.scalar_tensor_tensor(hid[:, s % 2, :], gelu[:, s % 2, :], w, up_ps[s % 2][:],
                                                             ALU.mult, ALU.mult)
                    ins.then_inc(hid_done, 1)
                    if s == LAG - 1 and not first:
                        for m in range(KH):
                            residual(it - 1, m)
                    if is_shared:
                        if first and n + 1 < CHUNKS:
                            shared_part(n + 1)
                    elif n + AHEAD < ROUTED:
                        quarter_part(it, n + AHEAD)
                    elif not last:
                        quarter_part(it + 1, n + AHEAD - ROUTED)
                    dve.wait_ge(hid_hi_done, it * STEPS + (s + 1))
                    lo_part(hid_lo[:, s % HB, :], hid[:, s % 2, :], hid_hi[:, s % HB, :]).then_inc(hid_lo_done, 1)
                    if not last:
                        if s == X_AT:
                            x_part(it + 1)
                        if s == HS_AT:
                            lora_part(it + 1)
                        if s == X1_AT:
                            x1_part(it + 1)

            dve.wait_ge(l0_hi_done, 1)
            lo_part(l0_lo[:], l0_w[:], l0_hi[:]).then_inc(l0_lo_done, 1)
            x_part(0)
            dve.wait_ge(small_loaded, 32)
            lora_part(0)
            shared_part(0)
            x1_part(0)
            quarter_part(0, 0)
            quarter_part(0, 1)
            pair(0, first=True)
            with dve.Fori(1, PAIRS - 1) as it:
                pair(it)
            pair(PAIRS - 1, last=True)
            for m in range(KH):
                residual(PAIRS - 1, m)

        @block.tensor
        def _(pe):
            def product(out, w, x, start, stop):
                (wh, wl), (xh, xl) = w, x
                nc.tensor.matmul(out, wl, xh, start=start, stop=False)
                nc.tensor.matmul(out, wh, xl, start=False, stop=False)
                return nc.tensor.matmul(out, wh, xh, start=False, stop=stop)

            def l0_cols(start, n):
                return l0_hi[:, start:start + n], l0_lo[:, start:start + n]

            def x_chunk(k):
                return x_hi[:, k * PT:(k + 1) * PT], x_lo[:, k * PT:(k + 1) * PT]

            def lora_down(it):
                pe.wait_ge(x_hi_done, it + 1)
                pe.wait_ge(x_lo_done, it + 1)
                if not isinstance(it, int) or it >= 1:
                    pe.wait_ge(x1_done, it * KH)
                for k in range(KH):
                    ins = product(l0_ps[0][:], l0_cols(A_AT + k * ER, ER), x_chunk(k), k == 0, k == KH - 1)
                ins.then_inc(lora_ready, 1)

            def layer0(it):
                pe.wait_ge(lora_hi_done, it + 1)
                pe.wait_ge(lora_lo_done, it + 1)
                for m in range(KH):
                    out = l0_ps[1 - m][:]
                    for k in range(KH):
                        product(out, l0_cols(BASE_AT + k * H + m * P, P), x_chunk(k), k == 0, False)
                    product(out, l0_cols(B_AT + m * P, P), (lora_hi[:], lora_lo[:]), False, True) \
                        .then_inc(l0_ready, 1)

            def gate_up(it, s, first):
                is_shared, n = KINDS[s]
                if is_shared:
                    if n == 0:
                        pe.wait_ge(x1_hi_done, it + 1)
                        pe.wait_ge(x1_lo_done, it + 1)
                    if first:
                        pe.wait_ge(s_hi_done, n + 1)
                        pe.wait_ge(s_lo_done, n + 1)
                    hi, lo, parts, width, at = s_hi[:, n, :], s_lo[:, n, :], 1, PT, 0
                else:
                    pe.wait_ge(w_hi_done, it * ROUTED + (n + 1))
                    pe.wait_ge(w_lo_done, it * ROUTED + (n + 1))
                    item = n // (2 * QUARTERS)
                    hi, lo, parts, width, at = w_hi[:, n % SPLIT, :], w_lo[:, n % SPLIT, :], QC, T, item * T
                for ps, which, ready, free in ((gate_ps, GATE, gate_ready, gelu_done), (up_ps, UP, up_ready, hid_done)):
                    if not first or s >= 2:
                        pe.wait_ge(free, it * STEPS + (s - 1))
                    for c in range(parts):
                        for k in range(KH):
                            w = slice(c * CW + which + k * P, c * CW + which + (k + 1) * P)
                            x = x1_cols(it, k * PT + at, width)
                            ins = product(ps[s % 2][:, c * width:(c + 1) * width], (hi[:, w], lo[:, w]),
                                          (x1_hi[:, x], x1_lo[:, x]), k == 0, k == KH - 1)
                    ins.then_inc(ready, 1)

            def down(it, s):
                is_shared, n = KINDS[s]
                pe.wait_ge(hid_hi_done, it * STEPS + (s + 1))
                pe.wait_ge(hid_lo_done, it * STEPS + (s + 1))
                if is_shared:
                    hi, lo, parts, width, at = s_hi[:, n, :], s_lo[:, n, :], 1, PT, 0
                else:
                    item = n // (2 * QUARTERS)
                    hi, lo, parts, width, at = w_hi[:, n % SPLIT, :], w_lo[:, n % SPLIT, :], QC, T, item * T
                for m in range(KH):
                    if s == 0 and (not isinstance(it, int) or it >= 1):
                        pe.wait_ge(y_done, it * KH + (m + 1 - KH))
                    for c in range(parts):
                        w = slice(c * CW + DOWN + m * P, c * CW + DOWN + (m + 1) * P)
                        h = slice(c * width, (c + 1) * width)
                        ins = product(out_ps[m][:, at:at + width], (hi[:, w], lo[:, w]),
                                      (hid_hi[:, s % HB, h], hid_lo[:, s % HB, h]), s == 0,
                                      s == STEPS - 1 and c == parts - 1)
                    if m == KH - 1:
                        ins.then_inc(down_done, 1)
                    elif s == STEPS - 1:
                        ins.then_inc(out_ready, 1)

            def pair(it, first=False, last=False):
                for s in range(STEPS):
                    gate_up(it, s, first)
                    if s >= LAG:
                        down(it, s - LAG)
                    elif not first:
                        down(it - 1, s - LAG + STEPS)
                    if not last:
                        if s == H_AT:
                            lora_down(it + 1)
                        if s == O_AT:
                            layer0(it + 1)

            pe.wait_ge(l0_hi_done, 1)
            pe.wait_ge(l0_lo_done, 1)
            lora_down(0)
            layer0(0)
            pair(0, first=True)
            with pe.Fori(1, PAIRS - 1) as it:
                pair(it)
            pair(PAIRS - 1, last=True)
            for s in range(STEPS - LAG, STEPS):
                down(PAIRS - 1, s)


def kernel(**inputs):
    import numpy as np
    import concourse.bacc as bacc
    from concourse.bass_utils import run_bass_kernel_spmd

    P = 128
    a = {k: np.asarray(v) for k, v in inputs.items()}
    B, T, H = a["x"].shape
    E, R, C = a["L0_cond_As"].shape
    I = a["L1_cond_shared_gate"].shape[1]
    K, CH, QUARTERS = H // P, I // P, 4

    def chunks(gate, up, down):
        n = gate.shape[0]
        g, u = (w.reshape(n, K, P, CH, P).transpose(0, 3, 2, 1, 4).reshape(n, CH, P, K * P) for w in (gate, up))
        return np.concatenate([g, u, down.reshape(n, CH, P, H)], axis=3)

    w = chunks(a["L1_cond_skill_gate"], a["L1_cond_skill_up"], a["L1_cond_skill_down"])
    QC = CH // QUARTERS
    w = w.reshape(E, QUARTERS, QC, P, 3 * H).transpose(0, 1, 3, 2, 4).reshape(E * QUARTERS * P, QC * 3 * H)
    s = chunks(*(a[f"L1_cond_shared_{n}"][None] for n in ("gate", "up", "down"))).reshape(CH * P, 3 * H)
    arrays = {
        "xT": a["x"].reshape(B * T, H).T,
        "cond": a["cond_8"],
        "condT": np.repeat(a["cond_8"].T, R, axis=0),
        "base_wT": a["L0_cond_W_base"].T,
        "base_b": a["L0_cond_b_base"].reshape(K, P).T,
        "lora_aT": a["L0_cond_As"].reshape(E * R, C).T,
        "lora_bT": a["L0_cond_Bs"].transpose(0, 2, 1).reshape(E * R, H),
        "experts": w,
        "shared": s,
    }
    arrays = {k: np.ascontiguousarray(v) for k, v in arrays.items()}
    nc = bacc.Bacc("TRN2", target_bir_lowering=False, num_devices=1)
    args = [nc.dram_tensor(k, v.shape, mybir.dt.from_np(v.dtype), kind="ExternalInput").ap()
            for k, v in arrays.items()]
    out = nc.dram_tensor("outT", (H, B * T), mybir.dt.float32, kind="ExternalOutput").ap()
    cond_resid_kernel(nc, *args, out)
    r = run_bass_kernel_spmd(nc, [arrays], core_ids=[0])
    return np.ascontiguousarray(r.results[0]["outT"].T).reshape(B, T, H)
```

```python
from contextlib import ExitStack

import concourse.bass as bass
from concourse import mybir


def cond_resid_kernel(nc, xT, small, base_wT, experts, shared, outT, B, E):
    F32, F32R, BF16, U32 = mybir.dt.float32, mybir.dt.float32r, mybir.dt.bfloat16, mybir.dt.uint32
    ALU, ACT, AX = mybir.AluOpType, mybir.ActivationFunctionType, mybir.AxisListType

    P = 128
    H, TOKENS = xT.shape
    KH = H // P
    T = TOKENS // B
    PT = 2 * T
    PAIRS = B // 2
    CHUNKS = shared.shape[0] // P
    CW = shared.shape[1]
    QUARTERS = experts.shape[0] // (E * P)
    QC = CHUNKS // QUARTERS
    QW = QC * CW
    ROUTED = 2 * 2 * QUARTERS
    PER_S = ROUTED // CHUNKS
    STEPS = CHUNKS + ROUTED
    LORA_SCALE = 32.0 / 16.0
    MIX = 1.0 / 12.0
    GATE, UP, DOWN = 0, H, 2 * H
    BIAS_AT, MIX_AT, LOGITS_AT = 0, KH, KH + B
    A_AT = LOGITS_AT + B * E
    B_AT = A_AT + H
    assert small.shape == (P, B_AT + H) and PT == 512 and QC * T == PT and CW == 3 * H

    LAG = 2
    HB = 3
    RAW = 4
    SPLIT = 4
    AHEAD = 2
    TOP = 8
    WARM = 20
    X_STEP, LORA_STEP, W_STEP, L0_STEP, X1_STEP = 3, 5, 7, 9, 11

    def step_of(r):
        return (PER_S + 1) * (r // PER_S) + 1 + r % PER_S

    def done_steps(it, s, back):
        n = it * STEPS + (s - back + 1)
        return None if isinstance(n, int) and n <= 0 else n

    KINDS = []
    for j in range(CHUNKS):
        KINDS += [(True, j)] + [(False, j * PER_S + i) for i in range(PER_S)]

    ctx = ExitStack()
    with ctx:
        def sb(name, shape, dt=F32):
            return ctx.enter_context(nc.sbuf_tensor(name, shape, dt))

        def sem(name):
            return ctx.enter_context(nc.semaphore(name))

        x_in = sb("x_in", [P, KH * PT])
        x_hi, x_lo = sb("x_hi", [P, KH * PT], F32R), sb("x_lo", [P, KH * PT], F32R)
        small_in = sb("small_in", [P, B_AT + H])
        bias, mix = small_in[:, BIAS_AT:MIX_AT], sb("mix", [P, B])
        a_raw, b_raw = small_in[:, A_AT:B_AT], small_in[:, B_AT:B_AT + H]
        a_hi, a_lo = sb("a_hi", [P, H], F32R), sb("a_lo", [P, H], F32R)
        mixed_b_hi, mixed_b_lo = sb("mixed_b_hi", [P, 2 * H], F32R), sb("mixed_b_lo", [P, 2 * H], F32R)
        base = sb("base", [P, KH * H])
        w0 = sb("w0", [P, 2, KH * H])
        mixed_b = w0[:, 0, :]
        w0_hi, w0_lo = sb("w0_hi", [P, 2, KH * H], F32R), sb("w0_lo", [P, 2, KH * H], F32R)
        x1 = sb("x1", [P, 2 * KH * PT])
        x1_hi, x1_lo = sb("x1_hi", [P, 2 * KH * PT], F32R), sb("x1_lo", [P, 2 * KH * PT], F32R)
        warm = sb("warm", [P, 4])
        logits = small_in[:, LOGITS_AT:A_AT].rearrange("p (b e) -> p b e", e=E)
        shifted, prob = sb("shifted", [P, B, E]), sb("prob", [P, B, E])
        top_logit, total, both = (sb(n, [P, B, 1]) for n in ("top_logit", "total", "both"))
        top = sb("top", [P, B, TOP])
        top_e = sb("top_e", [P, B, TOP], U32)
        share, share_mix, route_w = (sb(n, [P, B, 2]) for n in ("share", "share_mix", "route_w"))
        idle = sb("idle", [P, T], BF16)
        s_raw = sb("s_raw", [P, CW])
        s_hi, s_lo = sb("s_hi", [P, CHUNKS, CW], F32R), sb("s_lo", [P, CHUNKS, CW], F32R)
        w_raw = sb("w_raw", [P, RAW, QW])
        w_hi, w_lo = sb("w_hi", [P, SPLIT, QW], F32R), sb("w_lo", [P, SPLIT, QW], F32R)
        gelu = sb("gelu", [P, 2, PT])
        hid = sb("hid", [P, 2, PT])
        hid_hi, hid_lo = sb("hid_hi", [P, HB, PT], F32R), sb("hid_lo", [P, HB, PT], F32R)
        y = sb("y", [P, KH, PT])

        def bank(name):
            return ctx.enter_context(nc.psum_tensor(name, [P, PT], F32))

        gate_ps = [bank(f"gate_ps{i}") for i in range(2)]
        up_ps = [bank(f"up_ps{i}") for i in range(2)]
        out_ps = [bank(f"out_ps{m}") for m in range(KH)]
        l0_ps = [bank(f"l0_ps{m}") for m in range(2)]

        small_loaded = sem("small_loaded")
        base_loaded = sem("base_loaded")
        x_loaded = sem("x_loaded")
        s_loaded = sem("s_loaded")
        w_loaded = [sem(f"w_loaded{i}") for i in range(RAW)]
        idle_set = sem("idle_set")
        warm_set = sem("warm_set")
        routing = sem("routing")
        top_done = sem("top_done")
        chosen = sem("chosen")
        shifted_exp = sem("shifted_exp")
        mix_scaled = sem("mix_scaled")
        a_hi_done, a_lo_done = sem("a_hi_done"), sem("a_lo_done")
        x_hi_done, x_lo_done = sem("x_hi_done"), sem("x_lo_done")
        mixed_b_done = sem("mixed_b_done")
        mixed_b_hi_done, mixed_b_lo_done = sem("mixed_b_hi_done"), sem("mixed_b_lo_done")
        lora_ready = sem("lora_ready")
        w0_done, w0_hi_done, w0_lo_done = sem("w0_done"), sem("w0_hi_done"), sem("w0_lo_done")
        l0_ready = sem("l0_ready")
        x1_done, x1_hi_done, x1_lo_done = sem("x1_done"), sem("x1_hi_done"), sem("x1_lo_done")
        s_hi_done, s_lo_done = sem("s_hi_done"), sem("s_lo_done")
        w_hi_done, w_lo_done = sem("w_hi_done"), sem("w_lo_done")
        gate_ready, up_ready, gelu_done = sem("gate_ready"), sem("up_ready"), sem("gelu_done")
        hid_done, hid_hi_done, hid_lo_done = sem("hid_done"), sem("hid_hi_done"), sem("hid_lo_done")
        down_done = sem("down_done")
        out_ready = sem("out_ready")
        y_done = sem("y_done")
        last_stored = sem("last_stored")
        y_stored = [sem(f"y_stored{m}") for m in range(KH)]

        xT_v = xT.rearrange("(k p) t -> p k t", p=P)
        outT_v = outT.rearrange("(k p) t -> p k t", p=P)

        def parity(it):
            return it % 2 if isinstance(it, int) else it & 1

        def x1_cols(it, col, n):
            start = parity(it) * (KH * PT) + col
            return slice(start, start + n) if isinstance(start, int) else bass.ds(start, n)

        def cols(start, n):
            return slice(start, start + n) if isinstance(start, int) else bass.ds(start, n)

        block = ctx.enter_context(nc.Block())

        @block.sync
        def _(sp):
            numbers = top_e[:].rearrange("p b n -> p (b n)")

            def load_x(it):
                if not isinstance(it, int) or it >= 1:
                    sp.wait_ge(x1_done, it * KH)
                sp.dma_start(x_in[:].rearrange("p (k t) -> p k t", k=KH),
                             xT_v[:, :, cols(it * PT, PT)]).then_inc(x_loaded, 16)

            def load_shared(j):
                if j >= 1:
                    sp.wait_ge(s_lo_done, j)
                sp.dma_start(s_raw[:], shared[j * P:(j + 1) * P, :]).then_inc(s_loaded, 16)

            def load_pair(it, first=False, last=False):
                for r in range(ROUTED):
                    if r == RAW and not last:
                        load_x(it + 1)
                    item, choice = r // (2 * QUARTERS), r // QUARTERS % 2
                    if r % QUARTERS == 0:
                        if first:
                            sp.wait_ge(chosen, 2 if r == 0 else B)
                        e = sp.value_load(numbers[0:1, cols(it * (2 * TOP) + item * TOP + choice, 1)], min_val=0, max_val=E - 1)
                        row = sp.snap(e * (QUARTERS * P))
                    if not first or r >= RAW:
                        sp.wait_ge(w_lo_done, it * ROUTED + (r - RAW + 1))
                    sp.dma_start(w_raw[:, r % RAW, :], experts[bass.ds(row + (r % QUARTERS) * P, P), :]) \
                      .then_inc(w_loaded[r % RAW], 16)
                    if first and r % PER_S == PER_S - 1 and 1 + r // PER_S < CHUNKS:
                        load_shared(1 + r // PER_S)

            sp.dma_start(small_in[:], small).then_inc(small_loaded, 16)
            load_x(0)
            sp.dma_start(base[:].rearrange("p (k n) -> p k n", k=KH), base_wT.rearrange("(k p) n -> p k n", p=P)) \
              .then_inc(base_loaded, 16)
            load_shared(0)
            load_pair(0, first=True)
            with sp.Fori(1, PAIRS - 1) as it:
                load_pair(it)
            load_pair(PAIRS - 1, last=True)
            for m in range(KH):
                sp.wait_ge(y_done, (PAIRS - 1) * KH + m + 1)
                sp.dma_start(outT_v[:, m, (PAIRS - 1) * PT:], y[:, m, :]).then_inc(last_stored, 16)
            sp.wait_ge(last_stored, 16 * KH)

        @block.gpsimd
        def _(pool):
            nc.gpsimd.memset(warm[:], 0.0).then_inc(warm_set, 1)
            nc.gpsimd.memset(idle[:], 0.0).then_inc(idle_set, 1)
            pool.wait_ge(x_hi_done, 1)
            nc.gpsimd.tensor_tensor(x_lo[:], x_in[:], x_hi[:].bitcast(F32), ALU.subtract).then_inc(x_lo_done, 1)
            pool.wait_ge(s_hi_done, 1)
            nc.gpsimd.tensor_tensor(s_lo[:, 0, :], s_raw[:], s_hi[:, 0, :].bitcast(F32), ALU.subtract) \
              .then_inc(s_lo_done, 1)
            with pool.Fori(0, PAIRS - 1) as it:
                for m in range(KH):
                    pool.wait_ge(y_done, it * KH + (m + 1))
                    pool.dma_start(outT_v[:, m, bass.ds(it * PT, PT)], y[:, m, :]).then_inc(y_stored[m], 16)
            for m in range(KH):
                pool.wait_ge(y_stored[m], 16 * (PAIRS - 1))

        @block.scalar
        def _(act):
            def mixed_b_part(it):
                if not isinstance(it, int) or it >= 1:
                    act.wait_ge(lora_ready, it * 2)
                for i in range(2):
                    ins = nc.scalar.activation(mixed_b_hi[:, i * H:(i + 1) * H], b_raw, ACT.Copy,
                                               scale=mix[:, cols(it * 2 + i, 1)])
                ins.then_inc(mixed_b_hi_done, 1)

            def x_part(it):
                act.wait_ge(x_loaded, 16 * (it + 1))
                if not isinstance(it, int) or it >= 1:
                    act.wait_ge(l0_ready, it * KH)
                nc.scalar.activation(x_hi[:], x_in[:], ACT.Copy).then_inc(x_hi_done, 1)

            def w0_part(it, i):
                act.wait_ge(w0_done, it * 2 + (i + 1))
                if not isinstance(it, int) or it >= 1:
                    act.wait_ge(l0_ready, it * KH)
                nc.scalar.activation(w0_hi[:, i, :], w0[:, i, :], ACT.Copy).then_inc(w0_hi_done, 1)

            def x1_part(it, m):
                act.wait_ge(x1_done, it * KH + (m + 1))
                nc.scalar.activation(x1_hi[:, x1_cols(it, m * PT, PT)], x1[:, x1_cols(it, m * PT, PT)], ACT.Copy) \
                  .then_inc(x1_hi_done, 1)

            def shared_part(j):
                act.wait_ge(s_loaded, 16 * (j + 1))
                nc.scalar.activation(s_hi[:, j, :], s_raw[:], ACT.Copy).then_inc(s_hi_done, 1)

            def quarter_part(it, r, known_free=False):
                act.wait_ge(w_loaded[r % RAW], it * (16 * ROUTED // RAW) + 16 * (r // RAW + 1))
                if r >= SPLIT:
                    act.wait_ge(down_done, it * STEPS + (step_of(r - SPLIT) + 1))
                elif not known_free:
                    act.wait_ge(down_done, it * STEPS + (step_of(r - SPLIT + ROUTED) + 1 - STEPS))
                nc.scalar.activation(w_hi[:, r % SPLIT, :], w_raw[:, r % RAW, :], ACT.Copy).then_inc(w_hi_done, 1)

            def pair(it, first=False, last=False):
                for s, (is_shared, n) in enumerate(KINDS):
                    act.wait_ge(gate_ready, it * STEPS + (s + 1))
                    if not first or s >= 2:
                        act.wait_ge(hid_done, it * STEPS + (s - 1))
                    nc.scalar.activation(gelu[:, s % 2, :], gate_ps[s % 2][:], ACT.Gelu_apprx_tanh) \
                      .then_inc(gelu_done, 1)
                    if is_shared:
                        if first and n + 1 < CHUNKS:
                            shared_part(n + 1)
                    elif n + AHEAD < ROUTED:
                        quarter_part(it, n + AHEAD, known_free=first)
                    elif not last:
                        quarter_part(it + 1, n + AHEAD - ROUTED)
                    act.wait_ge(hid_done, it * STEPS + (s + 1))
                    if not first or s >= HB:
                        act.wait_ge(down_done, it * STEPS + (s - HB + 1))
                    nc.scalar.activation(hid_hi[:, s % HB, :], hid[:, s % 2, :], ACT.Copy).then_inc(hid_hi_done, 1)
                    if not last:
                        if s == X_STEP:
                            mixed_b_part(it + 1)
                            x_part(it + 1)
                        for i in range(2):
                            if s == W_STEP + i:
                                w0_part(it + 1, i)
                        for m in range(KH):
                            if s == X1_STEP + m:
                                x1_part(it + 1, m)

            act.wait_ge(warm_set, 1)
            nc.scalar.activation(warm[:, 0:1], warm[:, 1:2], ACT.Exp)
            act.wait_ge(small_loaded, 16)
            nc.scalar.activation(a_hi[:], a_raw, ACT.Copy).then_inc(a_hi_done, 1)
            act.wait_ge(mix_scaled, 1)
            mixed_b_part(0)
            act.wait_ge(routing, 2)
            nc.scalar.activation(shifted[:], shifted[:], ACT.Exp).then_inc(shifted_exp, 1)
            x_part(0)
            nc.scalar.activation(warm[:, 2:3], warm[:, 3:4], ACT.Gelu_apprx_tanh)
            w0_part(0, 0)
            w0_part(0, 1)
            shared_part(0)
            for m in range(KH):
                x1_part(0, m)
            quarter_part(0, 0, known_free=True)
            quarter_part(0, 1, known_free=True)
            pair(0, first=True)
            with act.Fori(1, PAIRS - 1) as it:
                pair(it)
            pair(PAIRS - 1, last=True)

        @block.vector
        def _(dve):
            route_n = [0]

            def link(ins):
                route_n[0] += 1
                ins.then_inc(routing, 1)
                dve.wait_ge(routing, route_n[0])

            def over_e(t):
                return t[:].broadcast_to([P, B, E])

            def route_shift():
                link(nc.vector.tensor_reduce(top_logit[:], logits, AX.X, ALU.max))
                link(nc.vector.tensor_tensor(shifted[:], logits, over_e(top_logit), ALU.subtract))

            def softmax():
                dve.wait_ge(shifted_exp, 1)
                link(nc.vector.tensor_reduce(total[:], shifted[:], AX.X, ALU.add))
                link(nc.vector.reciprocal(total[:], total[:]))
                link(nc.vector.tensor_tensor(prob[:], shifted[:], over_e(total), ALU.mult))

            def choose(items):
                for b in items:
                    nc.vector.max(top[:, b, :], prob[:, b, :]).then_inc(top_done, 1)
                for b in items:
                    dve.wait_ge(top_done, b + 1)
                    nc.vector.max_index(top_e[:, b, :], top[:, b, :], prob[:, b, :]).then_inc(chosen, 1)

            def weigh():
                link(nc.vector.tensor_tensor(both[:], top[:, :, 0:1], top[:, :, 1:2], ALU.add))
                link(nc.vector.reciprocal(both[:], both[:]))
                link(nc.vector.tensor_tensor(share[:], top[:, :, 0:2], both[:].broadcast_to([P, B, 2]), ALU.mult))
                link(nc.vector.tensor_scalar(share_mix[:], share[:], 1.0 - MIX, None, ALU.mult))
                link(nc.vector.scalar_tensor_tensor(route_w[:], share[:], MIX, share_mix[:], ALU.mult, ALU.add))

            weight_of = route_w[:].rearrange("p b n -> p (b n)")

            def lo_part(out, value, hi):
                return nc.vector.tensor_tensor(out, value, hi.bitcast(F32), ALU.subtract)

            def x_part(it):
                dve.wait_ge(x_hi_done, it + 1)
                lo_part(x_lo[:], x_in[:], x_hi[:]).then_inc(x_lo_done, 1)

            def mixed_b_make(it):
                if not isinstance(it, int) or it >= 1:
                    dve.wait_ge(w0_hi_done, it * 2)
                for i in range(2):
                    nc.vector.tensor_scalar(mixed_b[:, i * H:(i + 1) * H], b_raw, mix[:, cols(it * 2 + i, 1)], None,
                                            ALU.mult).then_inc(mixed_b_done, 1)

            def mixed_b_part(it):
                dve.wait_ge(mixed_b_done, it * 2 + 2)
                dve.wait_ge(mixed_b_hi_done, it + 1)
                lo_part(mixed_b_lo[:], mixed_b, mixed_b_hi[:]).then_inc(mixed_b_lo_done, 1)

            def w0_make(it, i):
                dve.wait_ge(lora_ready, it * 2 + (i + 1))
                nc.vector.tensor_tensor(w0[:, i, :], l0_ps[i][:], base[:], ALU.add).then_inc(w0_done, 1)

            def w0_part(it, i):
                dve.wait_ge(w0_hi_done, it * 2 + (i + 1))
                lo_part(w0_lo[:, i, :], w0[:, i, :], w0_hi[:, i, :]).then_inc(w0_lo_done, 1)

            def x1_part(it, m):
                dve.wait_ge(l0_ready, it * KH + (m + 1))
                nc.vector.scalar_tensor_tensor(x1[:, x1_cols(it, m * PT, PT)], l0_ps[m][:], bias[:, m:m + 1],
                                               x_in[:, m * PT:(m + 1) * PT], ALU.add, ALU.add).then_inc(x1_done, 1)
                dve.wait_ge(x1_hi_done, it * KH + (m + 1))
                lo_part(x1_lo[:, x1_cols(it, m * PT, PT)], x1[:, x1_cols(it, m * PT, PT)],
                        x1_hi[:, x1_cols(it, m * PT, PT)]).then_inc(x1_lo_done, 1)

            def shared_part(j):
                dve.wait_ge(s_hi_done, j + 1)
                lo_part(s_lo[:, j, :], s_raw[:], s_hi[:, j, :]).then_inc(s_lo_done, 1)

            def quarter_part(it, r):
                dve.wait_ge(w_hi_done, it * ROUTED + (r + 1))
                lo_part(w_lo[:, r % SPLIT, :], w_raw[:, r % RAW, :], w_hi[:, r % SPLIT, :]).then_inc(w_lo_done, 1)

            def residual(it, m):
                if m < KH - 1:
                    dve.wait_ge(out_ready, it * (KH - 1) + (m + 1))
                else:
                    dve.wait_ge(down_done, it * STEPS + STEPS)
                if not isinstance(it, int) or it >= 1:
                    dve.wait_ge(y_stored[m], 16 * it)
                nc.vector.tensor_tensor(y[:, m, :], out_ps[m][:], x1[:, x1_cols(it, m * PT, PT)], ALU.add) \
                  .then_inc(y_done, 1)

            def pair(it, first=False, last=False):
                for s, (is_shared, n) in enumerate(KINDS):
                    dve.wait_ge(gelu_done, it * STEPS + (s + 1))
                    dve.wait_ge(up_ready, it * STEPS + (s + 1))
                    if not first or s >= 2:
                        dve.wait_ge(hid_lo_done, it * STEPS + (s - 1))
                    if is_shared:
                        ins = nc.vector.tensor_tensor(hid[:, s % 2, :], gelu[:, s % 2, :], up_ps[s % 2][:], ALU.mult)
                    else:
                        w = weight_of[:, cols(it * 4 + n // QUARTERS, 1)]
                        ins = nc.vector.scalar_tensor_tensor(hid[:, s % 2, :], gelu[:, s % 2, :], w, up_ps[s % 2][:],
                                                             ALU.mult, ALU.mult)
                    ins.then_inc(hid_done, 1)
                    if s == LAG - 1 and not first:
                        for m in range(KH):
                            residual(it - 1, m)
                    if is_shared:
                        if first and n + 1 < CHUNKS:
                            shared_part(n + 1)
                    elif n + AHEAD < ROUTED:
                        quarter_part(it, n + AHEAD)
                    elif not last:
                        quarter_part(it + 1, n + AHEAD - ROUTED)
                    dve.wait_ge(hid_hi_done, it * STEPS + (s + 1))
                    lo_part(hid_lo[:, s % HB, :], hid[:, s % 2, :], hid_hi[:, s % HB, :]).then_inc(hid_lo_done, 1)
                    if not last:
                        if s == X_STEP:
                            mixed_b_make(it + 1)
                            mixed_b_part(it + 1)
                            x_part(it + 1)
                        for i in range(2):
                            if s == W_STEP + i:
                                w0_make(it + 1, i)
                                w0_part(it + 1, i)
                        for m in range(KH):
                            if s == X1_STEP + m:
                                x1_part(it + 1, m)

            dve.wait_ge(small_loaded, 16)
            nc.vector.tensor_scalar(mix[:], small_in[:, MIX_AT:LOGITS_AT], LORA_SCALE, None, ALU.mult) \
              .then_inc(mix_scaled, 1)
            dve.wait_ge(mix_scaled, 1)
            mixed_b_make(0)
            route_shift()
            dve.wait_ge(a_hi_done, 1)
            lo_part(a_lo[:], a_raw, a_hi[:]).then_inc(a_lo_done, 1)
            mixed_b_part(0)
            softmax()
            choose(range(2))
            dve.wait_ge(base_loaded, 16)
            w0_make(0, 0)
            w0_make(0, 1)
            w0_part(0, 0)
            w0_part(0, 1)
            choose(range(2, B))
            weigh()
            for m in range(KH):
                x1_part(0, m)
            quarter_part(0, 0)
            quarter_part(0, 1)
            pair(0, first=True)
            with dve.Fori(1, PAIRS - 1) as it:
                pair(it)
            pair(PAIRS - 1, last=True)
            for m in range(KH):
                residual(PAIRS - 1, m)

        @block.tensor
        def _(pe):
            def product(out, w, x, start, stop):
                (wh, wl), (xh, xl) = w, x
                nc.tensor.matmul(out, wl, xh, start=start, stop=False)
                nc.tensor.matmul(out, wh, xl, start=False, stop=False)
                return nc.tensor.matmul(out, wh, xh, start=False, stop=stop)

            def lora(it):
                pe.wait_ge(mixed_b_hi_done, it + 1)
                pe.wait_ge(mixed_b_lo_done, it + 1)
                if not isinstance(it, int) or it >= 1:
                    pe.wait_ge(x1_done, it * KH)
                for i in range(2):
                    b = slice(i * H, (i + 1) * H)
                    for k in range(KH):
                        a = slice(k * P, (k + 1) * P)
                        ins = product(l0_ps[i][:, k * H:(k + 1) * H], (a_hi[:, a], a_lo[:, a]),
                                      (mixed_b_hi[:, b], mixed_b_lo[:, b]), True, True)
                    ins.then_inc(lora_ready, 1)

            def layer0(it):
                pe.wait_ge(x_hi_done, it + 1)
                pe.wait_ge(x_lo_done, it + 1)
                for i in range(2):
                    pe.wait_ge(w0_hi_done, it * 2 + (i + 1))
                    pe.wait_ge(w0_lo_done, it * 2 + (i + 1))
                    for m in range(KH):
                        if i == 0 and m == 1:
                            pe.wait_ge(w0_done, it * 2 + 2)
                        for k in range(KH):
                            w = slice(k * H + m * P, k * H + (m + 1) * P)
                            x = slice(k * PT + i * T, k * PT + (i + 1) * T)
                            ins = product(l0_ps[m][:, i * T:(i + 1) * T], (w0_hi[:, i, w], w0_lo[:, i, w]),
                                          (x_hi[:, x], x_lo[:, x]), k == 0, k == KH - 1)
                        if i == 1:
                            ins.then_inc(l0_ready, 1)

            def gate_up(it, s, first):
                is_shared, n = KINDS[s]
                if is_shared:
                    if first:
                        pe.wait_ge(s_hi_done, n + 1)
                        pe.wait_ge(s_lo_done, n + 1)
                    hi, lo, parts, width, at = s_hi[:, n, :], s_lo[:, n, :], 1, PT, 0
                else:
                    pe.wait_ge(w_hi_done, it * ROUTED + (n + 1))
                    pe.wait_ge(w_lo_done, it * ROUTED + (n + 1))
                    item = n // (2 * QUARTERS)
                    hi, lo, parts, width, at = w_hi[:, n % SPLIT, :], w_lo[:, n % SPLIT, :], QC, T, item * T
                for ps, which, ready, free in ((gate_ps, GATE, gate_ready, gelu_done), (up_ps, UP, up_ready, hid_done)):
                    if not first or s >= 2:
                        pe.wait_ge(free, it * STEPS + (s - 1))
                    for c in range(parts):
                        for k in range(KH):
                            if s == 0 and which == GATE:
                                pe.wait_ge(x1_hi_done, it * KH + (k + 1))
                                pe.wait_ge(x1_lo_done, it * KH + (k + 1))
                            w = slice(c * CW + which + k * P, c * CW + which + (k + 1) * P)
                            x = x1_cols(it, k * PT + at, width)
                            ins = product(ps[s % 2][:, c * width:(c + 1) * width], (hi[:, w], lo[:, w]),
                                          (x1_hi[:, x], x1_lo[:, x]), k == 0, k == KH - 1)
                    ins.then_inc(ready, 1)

            def down(it, s):
                is_shared, n = KINDS[s]
                pe.wait_ge(hid_hi_done, it * STEPS + (s + 1))
                pe.wait_ge(hid_lo_done, it * STEPS + (s + 1))
                if is_shared:
                    hi, lo, parts, width, at = s_hi[:, n, :], s_lo[:, n, :], 1, PT, 0
                else:
                    item = n // (2 * QUARTERS)
                    hi, lo, parts, width, at = w_hi[:, n % SPLIT, :], w_lo[:, n % SPLIT, :], QC, T, item * T
                for m in range(KH):
                    if s == 0 and (not isinstance(it, int) or it >= 1):
                        pe.wait_ge(y_done, it * KH + (m + 1 - KH))
                    for c in range(parts):
                        w = slice(c * CW + DOWN + m * P, c * CW + DOWN + (m + 1) * P)
                        h = slice(c * width, (c + 1) * width)
                        ins = product(out_ps[m][:, at:at + width], (hi[:, w], lo[:, w]),
                                      (hid_hi[:, s % HB, h], hid_lo[:, s % HB, h]), s == 0,
                                      s == STEPS - 1 and c == parts - 1)
                    if m == KH - 1:
                        ins.then_inc(down_done, 1)
                    elif s == STEPS - 1:
                        ins.then_inc(out_ready, 1)

            def pair(it, first=False, last=False):
                for s in range(STEPS):
                    gate_up(it, s, first)
                    if s >= LAG:
                        down(it, s - LAG)
                    elif not first:
                        down(it - 1, s - LAG + STEPS)
                    if not last:
                        if s == LORA_STEP:
                            lora(it + 1)
                        if s == L0_STEP:
                            layer0(it + 1)

            pe.wait_ge(idle_set, 1)
            for _ in range(WARM):
                nc.tensor.matmul(out_ps[0][:, 0:T], idle[:, 0:P], idle[:], start=True, stop=True)
            pe.wait_ge(a_hi_done, 1)
            pe.wait_ge(a_lo_done, 1)
            lora(0)
            layer0(0)
            pair(0, first=True)
            with pe.Fori(1, PAIRS - 1) as it:
                pair(it)
            pair(PAIRS - 1, last=True)
            for s in range(STEPS - LAG, STEPS):
                down(PAIRS - 1, s)


def kernel(**inputs):
    import numpy as np
    import concourse.bacc as bacc
    from concourse.bass_utils import run_bass_kernel_spmd

    P = 128
    a = {k: np.asarray(v) for k, v in inputs.items()}
    B, T, H = a["x"].shape
    E, R, C = a["L0_cond_As"].shape
    I = a["L1_cond_shared_gate"].shape[1]
    K, CH, QUARTERS = H // P, I // P, 4

    def chunks(gate, up, down):
        n = gate.shape[0]
        g, u = (w.reshape(n, K, P, CH, P).transpose(0, 3, 2, 1, 4).reshape(n, CH, P, K * P) for w in (gate, up))
        return np.concatenate([g, u, down.reshape(n, CH, P, H)], axis=3)

    w = chunks(a["L1_cond_skill_gate"], a["L1_cond_skill_up"], a["L1_cond_skill_down"])
    QC = CH // QUARTERS
    w = w.reshape(E, QUARTERS, QC, P, 3 * H).transpose(0, 1, 3, 2, 4).reshape(E * QUARTERS * P, QC * 3 * H)
    s = chunks(*(a[f"L1_cond_shared_{n}"][None] for n in ("gate", "up", "down"))).reshape(CH * P, 3 * H)
    arrays = {
        "xT": a["x"].reshape(B * T, H).T,
        "small": np.concatenate([
            a["L0_cond_b_base"].reshape(K, P).T,
            np.repeat(a["cond_8"].T, R, axis=0),
            np.tile(a["cond_8"].reshape(1, B * E), (P, 1)),
            a["L0_cond_As"].reshape(E * R, C),
            a["L0_cond_Bs"].transpose(0, 2, 1).reshape(E * R, H),
        ], axis=1),
        "base_wT": a["L0_cond_W_base"].T,
        "experts": w,
        "shared": s,
    }
    arrays = {k: np.ascontiguousarray(v) for k, v in arrays.items()}
    nc = bacc.Bacc("TRN2", target_bir_lowering=False, num_devices=1)
    args = [nc.dram_tensor(k, v.shape, mybir.dt.from_np(v.dtype), kind="ExternalInput").ap()
            for k, v in arrays.items()]
    out = nc.dram_tensor("outT", (H, B * T), mybir.dt.float32, kind="ExternalOutput").ap()
    cond_resid_kernel(nc, *args, out, B, E)
    r = run_bass_kernel_spmd(nc, [arrays], core_ids=[0])
    return np.ascontiguousarray(r.results[0]["outT"].T).reshape(B, T, H)
```

```python
from contextlib import ExitStack

import concourse.bass as bass
from concourse import mybir


def cond_resid_kernel(nc, x, small, base_wT, experts, shared, outT, B, E):
    F32, F32R, BF16, U32 = mybir.dt.float32, mybir.dt.float32r, mybir.dt.bfloat16, mybir.dt.uint32
    ALU, ACT, AX = mybir.AluOpType, mybir.ActivationFunctionType, mybir.AxisListType

    P = 128
    H, T = x.shape[0] // B, x.shape[1]
    KH = H // P
    ITEMS = 2
    PT = ITEMS * T
    IC = KH * T
    PAIRS = B // ITEMS
    CHUNKS = shared.shape[0] // P
    CW = shared.shape[1]
    QUARTERS = experts.shape[0] // (E * P)
    QC = CHUNKS // QUARTERS
    QW = QC * CW
    ROUTED = ITEMS * 2 * QUARTERS
    PER_S = ROUTED // CHUNKS
    STEPS = CHUNKS + ROUTED
    LORA_SCALE = 32.0 / 16.0
    MIX = 1.0 / 12.0
    GATE, UP, DOWN = 0, H, 2 * H
    BIAS_AT, MIX_AT, LOGITS_AT = 0, KH, KH + B
    A_AT = LOGITS_AT + B * E
    B_AT = A_AT + H
    assert small.shape == (P, B_AT + H) and PT == 512 and QC * T == PT and CW == 3 * H

    LAG = 2
    HB = 3
    RAW = 4
    SPLIT = 4
    AHEAD = 2
    TOP = 8
    WARM = 18
    X_STEP, LORA_STEP, W_STEP, L0_STEP, X1_STEP = 3, 6, 8, 11, 13

    def step_of(r):
        return (PER_S + 1) * (r // PER_S) + 1 + r % PER_S

    def earlier(it):
        return not isinstance(it, int) or it >= 1

    KINDS = []
    for j in range(CHUNKS):
        KINDS += [(True, j)] + [(False, j * PER_S + i) for i in range(PER_S)]

    ctx = ExitStack()
    with ctx:
        def sb(name, shape, dt=F32):
            return ctx.enter_context(nc.sbuf_tensor(name, shape, dt))

        def sem(name):
            return ctx.enter_context(nc.semaphore(name))

        x_in = sb("x_in", [P, ITEMS * IC])
        x_hi, x_lo = sb("x_hi", [P, ITEMS * IC], F32R), sb("x_lo", [P, ITEMS * IC], F32R)
        small_in = sb("small_in", [P, B_AT + H])
        bias, mix = small_in[:, BIAS_AT:MIX_AT], sb("mix", [P, B])
        a_raw, b_raw = small_in[:, A_AT:B_AT], small_in[:, B_AT:B_AT + H]
        a_hi, a_lo = sb("a_hi", [P, H], F32R), sb("a_lo", [P, H], F32R)
        mixed_b_hi, mixed_b_lo = sb("mixed_b_hi", [P, 2 * H], F32R), sb("mixed_b_lo", [P, 2 * H], F32R)
        base = sb("base", [P, KH * H])
        w0 = sb("w0", [P, 2, KH * H])
        mixed_b = w0[:, 0, :]
        w0_hi, w0_lo = sb("w0_hi", [P, 2, KH * H], F32R), sb("w0_lo", [P, 2, KH * H], F32R)
        x1 = sb("x1", [P, 2 * ITEMS * IC])
        x1_hi, x1_lo = sb("x1_hi", [P, 2 * ITEMS * IC], F32R), sb("x1_lo", [P, 2 * ITEMS * IC], F32R)
        table = sb("table", [P, 4])
        logits = small_in[:, LOGITS_AT:A_AT].rearrange("p (b e) -> p b e", e=E)
        shifted, prob = sb("shifted", [P, B, E]), sb("prob", [P, B, E])
        top_logit, total, both = (sb(n, [P, B, 1]) for n in ("top_logit", "total", "both"))
        top = sb("top", [P, B, TOP])
        top_e = sb("top_e", [P, B, TOP], U32)
        share, share_mix, route_w = (sb(n, [P, B, 2]) for n in ("share", "share_mix", "route_w"))
        idle = sb("idle", [P, T], BF16)
        s_raw = sb("s_raw", [P, CW])
        s_hi, s_lo = sb("s_hi", [P, CHUNKS, CW], F32R), sb("s_lo", [P, CHUNKS, CW], F32R)
        w_raw = sb("w_raw", [P, RAW, QW])
        w_hi, w_lo = sb("w_hi", [P, SPLIT, QW], F32R), sb("w_lo", [P, SPLIT, QW], F32R)
        gelu = sb("gelu", [P, 2, PT])
        hid = sb("hid", [P, 2, PT])
        hid_hi, hid_lo = sb("hid_hi", [P, HB, PT], F32R), sb("hid_lo", [P, HB, PT], F32R)
        y = sb("y", [P, KH, PT])

        def bank(name):
            return ctx.enter_context(nc.psum_tensor(name, [P, PT], F32))

        gate_ps = [bank(f"gate_ps{i}") for i in range(2)]
        up_ps = [bank(f"up_ps{i}") for i in range(2)]
        out_ps = [bank(f"out_ps{m}") for m in range(KH)]
        l0_ps = [bank(f"l0_ps{i}") for i in range(ITEMS)]

        small_loaded = sem("small_loaded")
        base_loaded = sem("base_loaded")
        x_loaded = sem("x_loaded")
        s_loaded = sem("s_loaded")
        w_loaded = [sem(f"w_loaded{i}") for i in range(RAW)]
        idle_set = sem("idle_set")
        table_set = sem("table_set")
        routing = sem("routing")
        shifted_exp = sem("shifted_exp")
        top_done = sem("top_done")
        chosen = sem("chosen")
        mix_scaled = sem("mix_scaled")
        a_hi_done, a_lo_done = sem("a_hi_done"), sem("a_lo_done")
        x_hi_done, x_lo_done = sem("x_hi_done"), sem("x_lo_done")
        mixed_b_done = sem("mixed_b_done")
        mixed_b_hi_done, mixed_b_lo_done = sem("mixed_b_hi_done"), sem("mixed_b_lo_done")
        lora_ready = sem("lora_ready")
        w0_done, w0_hi_done, w0_lo_done = sem("w0_done"), sem("w0_hi_done"), sem("w0_lo_done")
        l0_ready = sem("l0_ready")
        x1_done, x1_hi_done, x1_lo_done = sem("x1_done"), sem("x1_hi_done"), sem("x1_lo_done")
        s_hi_done, s_lo_done = sem("s_hi_done"), sem("s_lo_done")
        w_hi_done, w_lo_done = sem("w_hi_done"), sem("w_lo_done")
        gate_ready, up_ready, gelu_done = sem("gate_ready"), sem("up_ready"), sem("gelu_done")
        hid_done, hid_hi_done, hid_lo_done = sem("hid_done"), sem("hid_hi_done"), sem("hid_lo_done")
        down_done = sem("down_done")
        out_ready = sem("out_ready")
        y_done = sem("y_done")
        y_stored = [sem(f"y_stored{m}") for m in range(KH)]

        x_v = x.rearrange("(b k p) t -> p (b k) t", p=P, k=KH)
        outT_v = outT.rearrange("(k p) t -> p k t", p=P)

        def parity(it):
            return it % 2 if isinstance(it, int) else it & 1

        def x1_item(tile, it, i):
            return tile[:, cols(parity(it) * (ITEMS * IC) + i * IC, IC)]

        def x1_chunk(tile, it, i, k):
            return tile[:, cols(parity(it) * (ITEMS * IC) + i * IC + k * T, T)]

        def x1_pair(tile, it, k):
            v = tile[:].rearrange("p (n t) -> p n t", t=T)
            start = parity(it) * (ITEMS * KH) + k
            if isinstance(start, int):
                return v[:, start:start + (ITEMS - 1) * KH + 1:KH, :]
            return v[:, bass.DynSlice(start, ITEMS, KH), :]

        def cols(start, n):
            return slice(start, start + n) if isinstance(start, int) else bass.ds(start, n)

        block = ctx.enter_context(nc.Block())

        @block.sync
        def _(sp):
            numbers = top_e[:].rearrange("p b n -> p (b n)")

            def load_x(it):
                if earlier(it):
                    sp.wait_ge(x1_done, it * ITEMS)
                sp.dma_start(x_in[:].rearrange("p (n t) -> p n t", t=T),
                             x_v[:, cols(it * (ITEMS * KH), ITEMS * KH), :]).then_inc(x_loaded, 16)

            def load_shared(j):
                if j >= 1:
                    sp.wait_ge(s_lo_done, j)
                sp.dma_start(s_raw[:], shared[j * P:(j + 1) * P, :]).then_inc(s_loaded, 16)

            def store_y(it):
                for m in range(KH):
                    sp.wait_ge(y_done, it * KH + (m + 1))
                    sp.dma_start(outT_v[:, m, cols(it * PT, PT)], y[:, m, :]).then_inc(y_stored[m], 16)

            def load_pair(it, first=False, last=False):
                for r in range(ROUTED):
                    if r == RAW + AHEAD and not first:
                        store_y(it - 1)
                    if r == RAW and not last:
                        load_x(it + 1)
                    item, choice = r // (2 * QUARTERS), r // QUARTERS % 2
                    if r % QUARTERS == 0:
                        if first:
                            sp.wait_ge(chosen, ITEMS if r == 0 else B)
                        e = sp.value_load(numbers[0:1, cols(it * (ITEMS * TOP) + item * TOP + choice, 1)],
                                          min_val=0, max_val=E - 1)
                        row = sp.snap(e * (QUARTERS * P))
                    if not first or r >= RAW:
                        sp.wait_ge(w_lo_done, it * ROUTED + (r - RAW + 1))
                    sp.dma_start(w_raw[:, r % RAW, :], experts[bass.ds(row + (r % QUARTERS) * P, P), :]) \
                      .then_inc(w_loaded[r % RAW], 16)
                    if first and r % PER_S == PER_S - 1 and 1 + r // PER_S < CHUNKS:
                        load_shared(1 + r // PER_S)

            sp.dma_start(small_in[:], small).then_inc(small_loaded, 16)
            load_x(0)
            sp.dma_start(base[:].rearrange("p (k n) -> p k n", k=KH), base_wT.rearrange("(k p) n -> p k n", p=P)) \
              .then_inc(base_loaded, 16)
            load_shared(0)
            load_pair(0, first=True)
            with sp.Fori(1, PAIRS - 1) as it:
                load_pair(it)
            load_pair(PAIRS - 1, last=True)
            store_y(PAIRS - 1)
            for m in range(KH):
                sp.wait_ge(y_stored[m], 16 * PAIRS)

        @block.gpsimd
        def _(pool):
            nc.gpsimd.memset(table[:], 0.0).then_inc(table_set, 1)
            nc.gpsimd.memset(idle[:], 0.0).then_inc(idle_set, 1)
            for i in range(ITEMS):
                pool.wait_ge(x_hi_done, i + 1)
                c = slice(i * IC, (i + 1) * IC)
                nc.gpsimd.tensor_tensor(x_lo[:, c], x_in[:, c], x_hi[:, c].bitcast(F32), ALU.subtract) \
                  .then_inc(x_lo_done, 1)
            pool.wait_ge(s_hi_done, 1)
            nc.gpsimd.tensor_tensor(s_lo[:, 0, :], s_raw[:], s_hi[:, 0, :].bitcast(F32), ALU.subtract) \
              .then_inc(s_lo_done, 1)

        @block.scalar
        def _(act):
            def mixed_b_part(it, i):
                if earlier(it):
                    act.wait_ge(lora_ready, it * ITEMS)
                nc.scalar.activation(mixed_b_hi[:, i * H:(i + 1) * H], b_raw, ACT.Copy,
                                     scale=mix[:, cols(it * ITEMS + i, 1)]).then_inc(mixed_b_hi_done, 1)

            def x_part(it, i):
                act.wait_ge(x_loaded, 16 * (it + 1))
                if earlier(it):
                    act.wait_ge(l0_ready, it * ITEMS)
                nc.scalar.activation(x_hi[:, i * IC:(i + 1) * IC], x_in[:, i * IC:(i + 1) * IC], ACT.Copy) \
                  .then_inc(x_hi_done, 1)

            def w0_part(it, i):
                act.wait_ge(w0_done, it * ITEMS + (i + 1))
                if earlier(it):
                    act.wait_ge(l0_ready, it * ITEMS)
                nc.scalar.activation(w0_hi[:, i, :], w0[:, i, :], ACT.Copy).then_inc(w0_hi_done, 1)

            def x1_part(it, i):
                act.wait_ge(x1_done, it * ITEMS + (i + 1))
                nc.scalar.activation(x1_item(x1_hi, it, i), x1_item(x1, it, i), ACT.Copy).then_inc(x1_hi_done, 1)

            def shared_part(j):
                act.wait_ge(s_loaded, 16 * (j + 1))
                nc.scalar.activation(s_hi[:, j, :], s_raw[:], ACT.Copy).then_inc(s_hi_done, 1)

            def quarter_part(it, r, known_free=False):
                act.wait_ge(w_loaded[r % RAW], it * (16 * ROUTED // RAW) + 16 * (r // RAW + 1))
                if r >= SPLIT:
                    act.wait_ge(down_done, it * STEPS + (step_of(r - SPLIT) + 1))
                elif not known_free:
                    act.wait_ge(down_done, it * STEPS + (step_of(r - SPLIT + ROUTED) + 1 - STEPS))
                nc.scalar.activation(w_hi[:, r % SPLIT, :], w_raw[:, r % RAW, :], ACT.Copy).then_inc(w_hi_done, 1)

            def pair(it, first=False, last=False):
                for s, (is_shared, n) in enumerate(KINDS):
                    act.wait_ge(gate_ready, it * STEPS + (s + 1))
                    if not first or s >= 2:
                        act.wait_ge(hid_done, it * STEPS + (s - 1))
                    nc.scalar.activation(gelu[:, s % 2, :], gate_ps[s % 2][:], ACT.Gelu_apprx_tanh) \
                      .then_inc(gelu_done, 1)
                    if is_shared:
                        if first and n + 1 < CHUNKS:
                            shared_part(n + 1)
                    elif n + AHEAD < ROUTED:
                        quarter_part(it, n + AHEAD, known_free=first)
                    elif not last:
                        quarter_part(it + 1, n + AHEAD - ROUTED)
                    act.wait_ge(hid_done, it * STEPS + (s + 1))
                    if not first or s >= HB:
                        act.wait_ge(down_done, it * STEPS + (s - HB + 1))
                    nc.scalar.activation(hid_hi[:, s % HB, :], hid[:, s % 2, :], ACT.Copy).then_inc(hid_hi_done, 1)
                    if not last:
                        for i in range(ITEMS):
                            if s == X_STEP + i:
                                mixed_b_part(it + 1, i)
                                x_part(it + 1, i)
                            if s == W_STEP + i:
                                w0_part(it + 1, i)
                            if s == X1_STEP + i:
                                x1_part(it + 1, i)

            act.wait_ge(table_set, 1)
            nc.scalar.activation(table[:, 0:1], table[:, 1:2], ACT.Exp)
            act.wait_ge(small_loaded, 16)
            nc.scalar.activation(a_hi[:], a_raw, ACT.Copy).then_inc(a_hi_done, 1)
            act.wait_ge(mix_scaled, 1)
            for i in range(ITEMS):
                mixed_b_part(0, i)
            x_part(0, 0)
            act.wait_ge(routing, 2)
            nc.scalar.activation(shifted[:], shifted[:], ACT.Exp).then_inc(shifted_exp, 1)
            x_part(0, 1)
            for i in range(ITEMS):
                w0_part(0, i)
            shared_part(0)
            nc.scalar.activation(table[:, 2:3], table[:, 3:4], ACT.Gelu_apprx_tanh)
            x1_part(0, 0)
            quarter_part(0, 0, known_free=True)
            x1_part(0, 1)
            quarter_part(0, 1, known_free=True)
            pair(0, first=True)
            with act.Fori(1, PAIRS - 1) as it:
                pair(it)
            pair(PAIRS - 1, last=True)

        @block.vector
        def _(dve):
            route_n = [0]

            def link(ins):
                route_n[0] += 1
                ins.then_inc(routing, 1)
                dve.wait_ge(routing, route_n[0])

            def over_e(t):
                return t[:].broadcast_to([P, B, E])

            def route_shift():
                link(nc.vector.tensor_reduce(top_logit[:], logits, AX.X, ALU.max))
                link(nc.vector.tensor_tensor(shifted[:], logits, over_e(top_logit), ALU.subtract))

            def softmax():
                dve.wait_ge(shifted_exp, 1)
                link(nc.vector.tensor_reduce(total[:], shifted[:], AX.X, ALU.add))
                link(nc.vector.reciprocal(total[:], total[:]))
                link(nc.vector.tensor_tensor(prob[:], shifted[:], over_e(total), ALU.mult))

            def choose(items):
                for b in items:
                    nc.vector.max(top[:, b, :], prob[:, b, :]).then_inc(top_done, 1)
                for b in items:
                    dve.wait_ge(top_done, b + 1)
                    nc.vector.max_index(top_e[:, b, :], top[:, b, :], prob[:, b, :]).then_inc(chosen, 1)

            def weigh():
                link(nc.vector.tensor_tensor(both[:], top[:, :, 0:1], top[:, :, 1:2], ALU.add))
                link(nc.vector.reciprocal(both[:], both[:]))
                link(nc.vector.tensor_tensor(share[:], top[:, :, 0:2], both[:].broadcast_to([P, B, 2]), ALU.mult))
                link(nc.vector.tensor_scalar(share_mix[:], share[:], 1.0 - MIX, None, ALU.mult))
                link(nc.vector.scalar_tensor_tensor(route_w[:], share[:], MIX, share_mix[:], ALU.mult, ALU.add))

            weight_of = route_w[:].rearrange("p b n -> p (b n)")

            def lo_part(out, value, hi):
                return nc.vector.tensor_tensor(out, value, hi.bitcast(F32), ALU.subtract)

            def x_part(it, i):
                dve.wait_ge(x_hi_done, it * ITEMS + (i + 1))
                c = slice(i * IC, (i + 1) * IC)
                lo_part(x_lo[:, c], x_in[:, c], x_hi[:, c]).then_inc(x_lo_done, 1)

            def mixed_b_make(it, i):
                if earlier(it):
                    dve.wait_ge(w0_hi_done, it * ITEMS)
                nc.vector.tensor_scalar(mixed_b[:, i * H:(i + 1) * H], b_raw, mix[:, cols(it * ITEMS + i, 1)], None,
                                        ALU.mult).then_inc(mixed_b_done, 1)

            def mixed_b_part(it, i):
                dve.wait_ge(mixed_b_done, it * ITEMS + (i + 1))
                dve.wait_ge(mixed_b_hi_done, it * ITEMS + (i + 1))
                c = slice(i * H, (i + 1) * H)
                lo_part(mixed_b_lo[:, c], mixed_b[:, c], mixed_b_hi[:, c]).then_inc(mixed_b_lo_done, 1)

            def w0_make(it, i):
                dve.wait_ge(lora_ready, it * ITEMS + (i + 1))
                nc.vector.tensor_tensor(w0[:, i, :], l0_ps[i][:], base[:], ALU.add).then_inc(w0_done, 1)

            def w0_part(it, i):
                dve.wait_ge(w0_hi_done, it * ITEMS + (i + 1))
                lo_part(w0_lo[:, i, :], w0[:, i, :], w0_hi[:, i, :]).then_inc(w0_lo_done, 1)

            def x1_make(it, i):
                dve.wait_ge(l0_ready, it * ITEMS + (i + 1))
                for m in range(KH):
                    ins = nc.vector.scalar_tensor_tensor(
                        x1_chunk(x1, it, i, m), l0_ps[i][:, m * T:(m + 1) * T], bias[:, m:m + 1],
                        x_in[:, i * IC + m * T:i * IC + (m + 1) * T], ALU.add, ALU.add)
                ins.then_inc(x1_done, 1)

            def x1_part(it, i):
                dve.wait_ge(x1_hi_done, it * ITEMS + (i + 1))
                lo_part(x1_item(x1_lo, it, i), x1_item(x1, it, i), x1_item(x1_hi, it, i)).then_inc(x1_lo_done, 1)

            def shared_part(j):
                dve.wait_ge(s_hi_done, j + 1)
                lo_part(s_lo[:, j, :], s_raw[:], s_hi[:, j, :]).then_inc(s_lo_done, 1)

            def quarter_part(it, r):
                dve.wait_ge(w_hi_done, it * ROUTED + (r + 1))
                lo_part(w_lo[:, r % SPLIT, :], w_raw[:, r % RAW, :], w_hi[:, r % SPLIT, :]).then_inc(w_lo_done, 1)

            def residual(it, m):
                if m < KH - 1:
                    dve.wait_ge(out_ready, it * (KH - 1) + (m + 1))
                else:
                    dve.wait_ge(down_done, it * STEPS + STEPS)
                if earlier(it):
                    dve.wait_ge(y_stored[m], 16 * it)
                nc.vector.tensor_tensor(y[:, m, :].rearrange("p (i t) -> p i t", t=T),
                                        out_ps[m][:].rearrange("p (i t) -> p i t", t=T), x1_pair(x1, it, m),
                                        ALU.add).then_inc(y_done, 1)

            def pair(it, first=False, last=False):
                for s, (is_shared, n) in enumerate(KINDS):
                    dve.wait_ge(gelu_done, it * STEPS + (s + 1))
                    dve.wait_ge(up_ready, it * STEPS + (s + 1))
                    if not first or s >= 2:
                        dve.wait_ge(hid_lo_done, it * STEPS + (s - 1))
                    if is_shared:
                        ins = nc.vector.tensor_tensor(hid[:, s % 2, :], gelu[:, s % 2, :], up_ps[s % 2][:], ALU.mult)
                    else:
                        w = weight_of[:, cols(it * 4 + n // QUARTERS, 1)]
                        ins = nc.vector.scalar_tensor_tensor(hid[:, s % 2, :], gelu[:, s % 2, :], w, up_ps[s % 2][:],
                                                             ALU.mult, ALU.mult)
                    ins.then_inc(hid_done, 1)
                    if s == LAG - 1 and not first:
                        for m in range(KH):
                            residual(it - 1, m)
                    if is_shared:
                        if first and n + 1 < CHUNKS:
                            shared_part(n + 1)
                    elif n + AHEAD < ROUTED:
                        quarter_part(it, n + AHEAD)
                    elif not last:
                        quarter_part(it + 1, n + AHEAD - ROUTED)
                    dve.wait_ge(hid_hi_done, it * STEPS + (s + 1))
                    lo_part(hid_lo[:, s % HB, :], hid[:, s % 2, :], hid_hi[:, s % HB, :]).then_inc(hid_lo_done, 1)
                    if not last:
                        for i in range(ITEMS):
                            if s == X_STEP + i:
                                mixed_b_make(it + 1, i)
                                mixed_b_part(it + 1, i)
                                x_part(it + 1, i)
                            if s == W_STEP + i:
                                w0_make(it + 1, i)
                                w0_part(it + 1, i)
                            if s == X1_STEP + i:
                                x1_make(it + 1, i)
                                x1_part(it + 1, i)

            dve.wait_ge(small_loaded, 16)
            nc.vector.tensor_scalar(mix[:], small_in[:, MIX_AT:LOGITS_AT], LORA_SCALE, None, ALU.mult) \
              .then_inc(mix_scaled, 1)
            dve.wait_ge(mix_scaled, 1)
            for i in range(ITEMS):
                mixed_b_make(0, i)
            dve.wait_ge(a_hi_done, 1)
            lo_part(a_lo[:], a_raw, a_hi[:]).then_inc(a_lo_done, 1)
            mixed_b_part(0, 0)
            route_shift()
            mixed_b_part(0, 1)
            softmax()
            choose(range(ITEMS))
            dve.wait_ge(base_loaded, 16)
            w0_make(0, 0)
            w0_make(0, 1)
            w0_part(0, 0)
            w0_part(0, 1)
            choose(range(ITEMS, B))
            for i in range(ITEMS):
                x1_make(0, i)
            for i in range(ITEMS):
                x1_part(0, i)
            quarter_part(0, 0)
            weigh()
            quarter_part(0, 1)
            pair(0, first=True)
            with dve.Fori(1, PAIRS - 1) as it:
                pair(it)
            pair(PAIRS - 1, last=True)
            for m in range(KH):
                residual(PAIRS - 1, m)

        @block.tensor
        def _(pe):
            def product(out, w, x, start, stop):
                (wh, wl), (xh, xl) = w, x
                nc.tensor.matmul(out, wl, xh, start=start, stop=False)
                nc.tensor.matmul(out, wh, xl, start=False, stop=False)
                return nc.tensor.matmul(out, wh, xh, start=False, stop=stop)

            def lora(it):
                if earlier(it):
                    pe.wait_ge(x1_done, it * ITEMS)
                for i in range(ITEMS):
                    pe.wait_ge(mixed_b_hi_done, it * ITEMS + (i + 1))
                    pe.wait_ge(mixed_b_lo_done, it * ITEMS + (i + 1))
                    b = slice(i * H, (i + 1) * H)
                    for k in range(KH):
                        a = slice(k * P, (k + 1) * P)
                        ins = product(l0_ps[i][:, k * H:(k + 1) * H], (a_hi[:, a], a_lo[:, a]),
                                      (mixed_b_hi[:, b], mixed_b_lo[:, b]), True, True)
                    ins.then_inc(lora_ready, 1)

            def layer0(it):
                for i in range(ITEMS):
                    pe.wait_ge(x_hi_done, it * ITEMS + (i + 1))
                    pe.wait_ge(x_lo_done, it * ITEMS + (i + 1))
                    pe.wait_ge(w0_hi_done, it * ITEMS + (i + 1))
                    pe.wait_ge(w0_lo_done, it * ITEMS + (i + 1))
                    for m in range(KH):
                        for k in range(KH):
                            w = slice(k * H + m * P, k * H + (m + 1) * P)
                            c = slice(i * IC + k * T, i * IC + (k + 1) * T)
                            ins = product(l0_ps[i][:, m * T:(m + 1) * T], (w0_hi[:, i, w], w0_lo[:, i, w]),
                                          (x_hi[:, c], x_lo[:, c]), k == 0, k == KH - 1)
                    ins.then_inc(l0_ready, 1)

            def step_products(it, s):
                is_shared, n = KINDS[s]
                if is_shared:
                    return s_hi[:, n, :], s_lo[:, n, :], [
                        (0, slice(0, PT), lambda k: (x1_pair(x1_hi, it, k), x1_pair(x1_lo, it, k)))]
                i = n // (2 * QUARTERS)
                return w_hi[:, n % SPLIT, :], w_lo[:, n % SPLIT, :], [
                    (c * CW, slice(c * T, (c + 1) * T),
                     lambda k: (x1_chunk(x1_hi, it, i, k), x1_chunk(x1_lo, it, i, k))) for c in range(QC)]

            def gate_up(it, s, first):
                is_shared, n = KINDS[s]
                if s == 0:
                    pe.wait_ge(x1_hi_done, it * ITEMS + ITEMS)
                    pe.wait_ge(x1_lo_done, it * ITEMS + ITEMS)
                if not is_shared:
                    pe.wait_ge(w_hi_done, it * ROUTED + (n + 1))
                    pe.wait_ge(w_lo_done, it * ROUTED + (n + 1))
                elif first:
                    pe.wait_ge(s_hi_done, n + 1)
                    pe.wait_ge(s_lo_done, n + 1)
                hi, lo, groups = step_products(it, s)
                for ps, which, ready, free in ((gate_ps, GATE, gate_ready, gelu_done), (up_ps, UP, up_ready, hid_done)):
                    if not first or s >= 2:
                        pe.wait_ge(free, it * STEPS + (s - 1))
                    for at, out, x in groups:
                        for k in range(KH):
                            w = slice(at + which + k * P, at + which + (k + 1) * P)
                            ins = product(ps[s % 2][:, out], (hi[:, w], lo[:, w]), x(k), k == 0, k == KH - 1)
                    ins.then_inc(ready, 1)

            def first_gate_up():
                pe.wait_ge(s_hi_done, 1)
                pe.wait_ge(s_lo_done, 1)
                for i in range(ITEMS):
                    pe.wait_ge(x1_hi_done, i + 1)
                    pe.wait_ge(x1_lo_done, i + 1)
                    for ps, which, ready in ((gate_ps, GATE, gate_ready), (up_ps, UP, up_ready)):
                        for k in range(KH):
                            w = slice(which + k * P, which + (k + 1) * P)
                            ins = product(ps[0][:, i * T:(i + 1) * T], (s_hi[:, 0, w], s_lo[:, 0, w]),
                                          (x1_chunk(x1_hi, 0, i, k), x1_chunk(x1_lo, 0, i, k)), k == 0, k == KH - 1)
                        if i == ITEMS - 1:
                            ins.then_inc(ready, 1)

            def down(it, s):
                is_shared, n = KINDS[s]
                pe.wait_ge(hid_hi_done, it * STEPS + (s + 1))
                pe.wait_ge(hid_lo_done, it * STEPS + (s + 1))
                if is_shared:
                    hi, lo, parts, width, at = s_hi[:, n, :], s_lo[:, n, :], 1, PT, 0
                else:
                    i = n // (2 * QUARTERS)
                    hi, lo, parts, width, at = w_hi[:, n % SPLIT, :], w_lo[:, n % SPLIT, :], QC, T, i * T
                for m in range(KH):
                    if s == 0 and earlier(it):
                        pe.wait_ge(y_done, it * KH + (m + 1 - KH))
                    for c in range(parts):
                        w = slice(c * CW + DOWN + m * P, c * CW + DOWN + (m + 1) * P)
                        h = slice(c * width, (c + 1) * width)
                        ins = product(out_ps[m][:, at:at + width], (hi[:, w], lo[:, w]),
                                      (hid_hi[:, s % HB, h], hid_lo[:, s % HB, h]), s == 0,
                                      s == STEPS - 1 and c == parts - 1)
                    if m == KH - 1:
                        ins.then_inc(down_done, 1)
                    elif s == STEPS - 1:
                        ins.then_inc(out_ready, 1)

            def pair(it, first=False, last=False):
                for s in range(STEPS):
                    if first and s == 0:
                        first_gate_up()
                    else:
                        gate_up(it, s, first)
                    if s >= LAG:
                        down(it, s - LAG)
                    elif not first:
                        down(it - 1, s - LAG + STEPS)
                    if not last:
                        if s == LORA_STEP:
                            lora(it + 1)
                        if s == L0_STEP:
                            layer0(it + 1)

            pe.wait_ge(idle_set, 1)
            for _ in range(WARM):
                nc.tensor.matmul(out_ps[0][:, 0:T], idle[:, 0:P], idle[:], start=True, stop=True)
            pe.wait_ge(a_hi_done, 1)
            pe.wait_ge(a_lo_done, 1)
            lora(0)
            layer0(0)
            pair(0, first=True)
            with pe.Fori(1, PAIRS - 1) as it:
                pair(it)
            pair(PAIRS - 1, last=True)
            for s in range(STEPS - LAG, STEPS):
                down(PAIRS - 1, s)


def kernel(**inputs):
    import numpy as np
    import concourse.bacc as bacc
    from concourse.bass_utils import run_bass_kernel_spmd

    P = 128
    a = {k: np.asarray(v) for k, v in inputs.items()}
    B, T, H = a["x"].shape
    E, R, C = a["L0_cond_As"].shape
    I = a["L1_cond_shared_gate"].shape[1]
    K, CH, QUARTERS = H // P, I // P, 4

    def chunks(gate, up, down):
        n = gate.shape[0]
        g, u = (w.reshape(n, K, P, CH, P).transpose(0, 3, 2, 1, 4).reshape(n, CH, P, K * P) for w in (gate, up))
        return np.concatenate([g, u, down.reshape(n, CH, P, H)], axis=3)

    w = chunks(a["L1_cond_skill_gate"], a["L1_cond_skill_up"], a["L1_cond_skill_down"])
    QC = CH // QUARTERS
    w = w.reshape(E, QUARTERS, QC, P, 3 * H).transpose(0, 1, 3, 2, 4).reshape(E * QUARTERS * P, QC * 3 * H)
    s = chunks(*(a[f"L1_cond_shared_{n}"][None] for n in ("gate", "up", "down"))).reshape(CH * P, 3 * H)
    arrays = {
        "x": a["x"].transpose(0, 2, 1).reshape(B * H, T),
        "small": np.concatenate([
            a["L0_cond_b_base"].reshape(K, P).T,
            np.repeat(a["cond_8"].T, R, axis=0),
            np.tile(a["cond_8"].reshape(1, B * E), (P, 1)),
            a["L0_cond_As"].reshape(E * R, C),
            a["L0_cond_Bs"].transpose(0, 2, 1).reshape(E * R, H),
        ], axis=1),
        "base_wT": a["L0_cond_W_base"].T,
        "experts": w,
        "shared": s,
    }
    arrays = {k: np.ascontiguousarray(v) for k, v in arrays.items()}
    nc = bacc.Bacc("TRN2", target_bir_lowering=False, num_devices=1)
    args = [nc.dram_tensor(k, v.shape, mybir.dt.from_np(v.dtype), kind="ExternalInput").ap()
            for k, v in arrays.items()]
    out = nc.dram_tensor("outT", (H, B * T), mybir.dt.float32, kind="ExternalOutput").ap()
    cond_resid_kernel(nc, *args, out, B, E)
    r = run_bass_kernel_spmd(nc, [arrays], core_ids=[0])
    return np.ascontiguousarray(r.results[0]["outT"].T).reshape(B, T, H)
```
